# Optimizing a Trainium2 kernel written in Bass

```python
import numpy as np
import jax
import jax.numpy as jnp

def _softmax(x, axis=-1):
    return jax.nn.softmax(x, axis=axis)

def _gelu(x):
    return jax.nn.gelu(x, approximate=True)

def _silu(x):
    return jax.nn.silu(x)

def _sigmoid(x):
    return jax.nn.sigmoid(x)

def _layernorm(x, axis=-1, eps=1e-05):
    m = jnp.mean(x, axis=axis, keepdims=True)
    v = jnp.var(x, axis=axis, keepdims=True)
    return (x - m) / jnp.sqrt(v + eps)

def _scatter_add(tgt, idx, src, axis=0):
    return tgt.at[idx].add(src)

def _segment_sum(src, seg, n):
    return jax.ops.segment_sum(src, seg, n)
kernel_name = 'mk_adj_resnorm_d2_adj_r2_9ab0fc'

def setup_inputs(seed: int=0):
    np.random.seed(seed)
    _w = jnp.asarray

    def _rec_inputs():
        import jax
        import jax.numpy as jnp
        _gk = jax.random.key(seed)
        x = -0.003407 + 1.001 * jax.random.normal(jax.random.fold_in(_gk, 1), (32, 256, 64), jnp.float32)
        _a = jax.random.bernoulli(jax.random.fold_in(_gk, 2), 0.0625, (32, 256, 256))
        _a = jnp.logical_or(_a, jnp.swapaxes(_a, -1, -2))
        _a = jnp.logical_or(_a, jnp.eye(256, dtype=bool))
        _af = _a.astype(jnp.float32)
        adj = _af
        return (x, adj)
    x, adj = _rec_inputs()

    def _L0_gnn_setup():
        import jax, jax.numpy as jnp
        import numpy as np
        B, N, DIN, DOUT = (8, 128, 64, 64)
        AVG_D_LOG = 4.86
        EPS = 1e-05
        NEG_BIG = 1000000000.0
        N_AGG, N_SCALE = (4, 3)

        def _pna_forward(x, adj, W_pre, b_pre, W_post, b_post):
            n = adj.shape[1]
            h_i = jnp.broadcast_to(x[:, :, None, :], (x.shape[0], n, n, x.shape[-1]))
            h_j = jnp.broadcast_to(x[:, None, :, :], (x.shape[0], n, n, x.shape[-1]))
            h_cat = jnp.concatenate([h_i, h_j], axis=-1)
            h_mod = jnp.einsum('bnme,ed->bnmd', h_cat, W_pre) + b_pre
            deg = adj.sum(-1)
            deg_safe = jnp.maximum(deg, 1.0)[..., None]
            mask = (adj > 0)[..., None]
            s1 = jnp.einsum('bnm,bnmd->bnd', adj, h_mod)
            mean = s1 / deg_safe
            s2 = jnp.einsum('bnm,bnmd->bnd', adj, h_mod * h_mod)
            var = jax.nn.relu(s2 / deg_safe - mean * mean)
            std = jnp.sqrt(var + EPS)
            mx = jnp.max(jnp.where(mask, h_mod, -NEG_BIG), axis=2)
            mn = jnp.min(jnp.where(mask, h_mod, NEG_BIG), axis=2)
            m = jnp.concatenate([mean, mx, mn, std], axis=-1)
            log_deg = jnp.log(deg + 1.0)[..., None]
            amp = m * (log_deg / AVG_D_LOG)
            att = m * (AVG_D_LOG / jnp.maximum(log_deg, EPS))
            m_all = jnp.concatenate([m, amp, att], axis=-1)
            m_cat = jnp.concatenate([x, m_all], axis=-1)
            return jnp.einsum('bne,ed->bnd', m_cat, W_post) + b_post
        key = jax.random.key(seed)
        k1, k2, k3, k4, k5, k6 = jax.random.split(key, 6)
        inp = jax.random.normal(k1, (B, N, DIN), dtype=jnp.float32)
        adj = jax.random.randint(k2, (B, N, N), 0, 2).astype(jnp.float32)
        W_pre = jax.random.normal(k3, (2 * DIN, DIN), dtype=jnp.float32) / np.sqrt(2 * DIN)
        b_pre = jnp.zeros((DIN,), dtype=jnp.float32)
        post_in = (N_AGG * N_SCALE + 1) * DIN
        W_post = jax.random.normal(k4, (post_in, DOUT), dtype=jnp.float32) / np.sqrt(post_in)
        b_post = jnp.zeros((DOUT,), dtype=jnp.float32)
        return {'input': inp, 'adj': adj, 'W_pre': W_pre, 'b_pre': b_pre, 'W_post': W_post, 'b_post': b_post}
    _L0_gnn_all = _L0_gnn_setup()
    _L0_gnn_in = {k: v for k, v in _L0_gnn_all.items() if k in ('W_pre', 'b_pre', 'W_post', 'b_post')}
    del _L0_gnn_all

    def _L1_gnn_setup():
        import jax, jax.numpy as jnp
        import numpy as np
        B, N, H = (4, 2048, 64)
        key = jax.random.key(seed)
        ks = jax.random.split(key, 12)
        s = 1.0 / np.sqrt(H)
        h = jax.random.normal(ks[0], (B, N, H), dtype=jnp.float32)
        A = jax.random.uniform(ks[1], (B, N, N), dtype=jnp.float32)
        W1 = jax.random.normal(ks[2], (H, H), dtype=jnp.float32) * s
        b1 = jnp.zeros((H,), dtype=jnp.float32)
        W2 = jax.random.normal(ks[3], (H, H), dtype=jnp.float32) * s
        b2 = jnp.zeros((H,), dtype=jnp.float32)
        W_ih = jax.random.normal(ks[4], (3 * H, H), dtype=jnp.float32) * s
        b_ih = jnp.zeros((3 * H,), dtype=jnp.float32)
        W_hh = jax.random.normal(ks[5], (3 * H, H), dtype=jnp.float32) * s
        b_hh = jnp.zeros((3 * H,), dtype=jnp.float32)
        return {'h': h, 'A': A, 'W1': W1, 'b1': b1, 'W2': W2, 'b2': b2, 'W_ih': W_ih, 'b_ih': b_ih, 'W_hh': W_hh, 'b_hh': b_hh}
    _L1_gnn_all = _L1_gnn_setup()
    _L1_gnn_in = {k: v for k, v in _L1_gnn_all.items() if k in ('W1', 'b1', 'W2', 'b2', 'W_ih', 'b_ih', 'W_hh', 'b_hh')}
    del _L1_gnn_all
    return {'x': x, 'adj': adj, 'L0_gnn_W_pre': _L0_gnn_in['W_pre'], 'L0_gnn_b_pre': _L0_gnn_in['b_pre'], 'L0_gnn_W_post': _L0_gnn_in['W_post'], 'L0_gnn_b_post': _L0_gnn_in['b_post'], 'L1_gnn_W1': _L1_gnn_in['W1'], 'L1_gnn_b1': _L1_gnn_in['b1'], 'L1_gnn_W2': _L1_gnn_in['W2'], 'L1_gnn_b2': _L1_gnn_in['b2'], 'L1_gnn_W_ih': _L1_gnn_in['W_ih'], 'L1_gnn_b_ih': _L1_gnn_in['b_ih'], 'L1_gnn_W_hh': _L1_gnn_in['W_hh'], 'L1_gnn_b_hh': _L1_gnn_in['b_hh']}

def reference(x, adj, L0_gnn_W_pre, L0_gnn_b_pre, L0_gnn_W_post, L0_gnn_b_post, L1_gnn_W1, L1_gnn_b1, L1_gnn_W2, L1_gnn_b2, L1_gnn_W_ih, L1_gnn_b_ih, L1_gnn_W_hh, L1_gnn_b_hh):
    import jax
    import jax.numpy as jnp

    def _L0_gnn_ref(input, adj, W_pre, b_pre, W_post, b_post):
        import jax, jax.numpy as jnp
        import numpy as np
        B, N, DIN, DOUT = (8, 128, 64, 64)
        AVG_D_LOG = 4.86
        EPS = 1e-05
        NEG_BIG = 1000000000.0
        N_AGG, N_SCALE = (4, 3)

        def _pna_forward(x, adj, W_pre, b_pre, W_post, b_post):
            n = adj.shape[1]
            h_i = jnp.broadcast_to(x[:, :, None, :], (x.shape[0], n, n, x.shape[-1]))
            h_j = jnp.broadcast_to(x[:, None, :, :], (x.shape[0], n, n, x.shape[-1]))
            h_cat = jnp.concatenate([h_i, h_j], axis=-1)
            h_mod = jnp.einsum('bnme,ed->bnmd', h_cat, W_pre) + b_pre
            deg = adj.sum(-1)
            deg_safe = jnp.maximum(deg, 1.0)[..., None]
            mask = (adj > 0)[..., None]
            s1 = jnp.einsum('bnm,bnmd->bnd', adj, h_mod)
            mean = s1 / deg_safe
            s2 = jnp.einsum('bnm,bnmd->bnd', adj, h_mod * h_mod)
            var = jax.nn.relu(s2 / deg_safe - mean * mean)
            std = jnp.sqrt(var + EPS)
            mx = jnp.max(jnp.where(mask, h_mod, -NEG_BIG), axis=2)
            mn = jnp.min(jnp.where(mask, h_mod, NEG_BIG), axis=2)
            m = jnp.concatenate([mean, mx, mn, std], axis=-1)
            log_deg = jnp.log(deg + 1.0)[..., None]
            amp = m * (log_deg / AVG_D_LOG)
            att = m * (AVG_D_LOG / jnp.maximum(log_deg, EPS))
            m_all = jnp.concatenate([m, amp, att], axis=-1)
            m_cat = jnp.concatenate([x, m_all], axis=-1)
            return jnp.einsum('bne,ed->bnd', m_cat, W_post) + b_post
        return _pna_forward(input, adj, W_pre, b_pre, W_post, b_post)

    def _L1_gnn_ref(h, A, W1, b1, W2, b2, W_ih, b_ih, W_hh, b_hh):
        import jax, jax.numpy as jnp
        import numpy as np
        B, N, H = (4, 2048, 64)
        m = jax.nn.relu(jnp.einsum('bnh,hk->bnk', h, W1) + b1)
        m = jax.nn.relu(jnp.einsum('bnh,hk->bnk', m, W2) + b2)
        msg = jax.nn.relu(jnp.einsum('bij,bjh->bih', A, m))
        gi = jnp.einsum('bnh,gh->bng', msg, W_ih) + b_ih
        gh = jnp.einsum('bnh,gh->bng', h, W_hh) + b_hh
        i_r, i_z, i_n = jnp.split(gi, 3, axis=-1)
        h_r, h_z, h_n = jnp.split(gh, 3, axis=-1)
        r = jax.nn.sigmoid(i_r + h_r)
        z = jax.nn.sigmoid(i_z + h_z)
        n = jnp.tanh(i_n + r * h_n)
        return (1.0 - z) * n + z * h
    x = _layernorm(x + _L0_gnn_ref(x, adj, L0_gnn_W_pre, L0_gnn_b_pre, L0_gnn_W_post, L0_gnn_b_post), axis=-1)
    x = _layernorm(x + _L1_gnn_ref(x, adj, L1_gnn_W1, L1_gnn_b1, L1_gnn_W2, L1_gnn_b2, L1_gnn_W_ih, L1_gnn_b_ih, L1_gnn_W_hh, L1_gnn_b_hh), axis=-1)
    return x

_drawn_inputs = setup_inputs


def setup_inputs(seed=0):
    import zlib

    import numpy as np

    out = dict(_drawn_inputs(seed))
    spreads = {'L0_gnn_b_pre': (0.0, 0.1),
     'L0_gnn_b_post': (0.0, 0.1),
     'L1_gnn_b1': (0.0, 0.1),
     'L1_gnn_b2': (0.0, 0.1),
     'L1_gnn_b_ih': (0.0, 0.684),
     'L1_gnn_b_hh': (0.0, 0.8)}
    factors = {}
    for name, (base, spread) in spreads.items():
        noise = np.random.default_rng([zlib.crc32(name.encode()), seed]).standard_normal(out[name].shape)
        drawn = base * np.exp(spread * noise) if base else spread * noise
        out[name] = jnp.asarray(drawn.astype(out[name].dtype))
    for name, factor in factors.items():
        out[name] = (out[name] * factor).astype(out[name].dtype)
    return out
```

```python
from contextlib import ExitStack

import numpy as np

import concourse.bass as bass
from concourse import mybir
from concourse.alu_op_type import AluOpType as ALU

F32 = mybir.dt.float32
BF16 = mybir.dt.bfloat16
ACT = mybir.ActivationFunctionType
AX_X = mybir.AxisListType.X

B, N, D = 32, 256, 64
P = 128
H = N // P
T = B * H
GS = 5
PAT = 1 << GS
PARTS = 3
KR = PARTS * PAT
GT = 4
NT = 13
NG = NT * GT
TA = 8
NEG = -1.0e9
EPS = 1e-5
AVG = 4.86
SPANS = [g for g in range(NG) if GS * g < P <= GS * g + GS - 1]
QB = 4
TB = QB * H


def match_blocks():
    blocks = []
    for g in range(NG):
        for half in range(H):
            if any(half * P <= m < (half + 1) * P for m in range(GS * g, min(GS * g + GS, N))):
                blocks.append((g, half))
    return blocks


BLOCKS = match_blocks()


def match_constants():
    w = np.zeros((P, len(BLOCKS), KR), np.float32)
    for i, (g, half) in enumerate(BLOCKS):
        for j in range(GS):
            m = GS * g + j - half * P
            if 0 <= m < P and GS * g + j < N:
                for r in range(KR):
                    w[m, i, r] = 1.0 if (r % PAT) >> j & 1 else -1.0
    bias = np.array([[1.0 - bin(r % PAT).count("1")] for r in range(KR)], np.float32)
    return w, bias


def steps(has_u, has_x, has_adj, has_next):
    s = [[] for _ in range(NT)]
    for t in range(NT - 1):
        s[t].append(("M", t + 1))
    if has_next:
        s[NT - 1].append(("M0", 0))
    if has_adj:
        s[1].insert(0, ("AT", 0))
        s[6].insert(0, ("SQ", 0))
        s[10].append(("STD", 0))
        s[11].append(("MST", 0))
    if has_u:
        s[2].insert(0, ("U", 0))
    if has_x:
        s[3].insert(0, ("XT", 0))
        s[4].insert(0, ("V", 0))
        s[8].insert(0, ("TPA", 0))
        s[9].insert(0, ("TPB", 0))
    return s


PROLOGUE = 12
FULL = NT + 8


def pool_base(j, b):
    if isinstance(j, int) and 2 * j + b == 0:
        return PROLOGUE
    if isinstance(j, int) and 2 * j + b == B - 1:
        return pool_base(j, 0) + FULL - 4
    return (j * 2 + b) * FULL + (PROLOGUE - 1)


def iteration_flags(j, b):
    if not isinstance(j, int):
        return True, True, True, True
    g = 2 * j + b
    return g > 0, g < B - 2, g < B - 1, g < B - 1


def pool_order(j, b):
    plan = steps(*iteration_flags(j, b))
    base = pool_base(j, b)
    parity = base % 2 if isinstance(j, int) else (b * FULL + PROLOGUE - 1) % 2
    at, order = 0, []
    for tile in plan:
        row = []
        for name, t in tile:
            if name == "STD":
                row.append((name, t, None, None))
                continue
            row.append((name, t, base + at, (parity + at) % 2))
            at += 1
        order.append(row)
    where = {(name, t): k for row in order for name, t, k, _ in row}
    return order, where


POOL_STEPS = pool_base(B // 2 - 1, 1) + FULL - 8 + 1


def build(nc, x, adj, w_pre, b_pre, w_post, b_post, w1, b1, w2, b2, w_ih, b_ih, w_hh, b_hh,
          ident_c, match_c, mbias_c, out):
    ctx = ExitStack()
    with ctx:
        def sb(name, shape, dt=F32):
            return ctx.enter_context(nc.sbuf_tensor(name, shape, dt))

        def sem(name):
            return ctx.enter_context(nc.semaphore(name))

        ident = sb("ident", [P, P])
        match = sb("match", [P, len(BLOCKS), KR], BF16)
        mbias = sb("mbias", [KR, 1])
        eps_col = sb("eps_col", [P, 1])
        m_half = sb("m_half", [P, TB])
        ones_col = sb("ones_col", [P, 1], BF16)
        ones_row = sb("ones_row", [1, P])
        wc_pm = sb("wc_pm", [D, 2 * D])
        w_tok = sb("w_tok", [D + 1, 2 * D])
        w_ext = sb("w_ext", [P, 3 * D])
        w_ms = sb("w_ms", [P, 3 * D])
        w_sum = sb("w_sum", [D, 3 * D])
        w_x = sb("w_x", [D + 1, 3 * D])
        wa_t = sb("wa_t", [D, D + 1])
        w1_s = sb("w1_s", [P, D])
        b1_s = sb("b1_s", [D, 1])
        w2_s = sb("w2_s", [D + 1, D])
        w_gru = sb("w_gru", [P, 4 * D])
        gru_raw = sb("gru_raw", [96, 2, 2, D])
        b_gru = sb("b_gru", [1, 4 * D])
        b_raw = sb("b_raw", [1, 2, 3 * D])

        adjt_all = sb("adjt_all", [P, B, H * N], BF16)
        u_all = sb("u_all", [P, T, 3 * D])
        deg_all = sb("deg_all", [P, T])

        adj_in = [sb(f"adj_in{i}", [P, H, N]) for i in range(2)]
        x_tok = [sb(f"x_tok{i}", [P, H, D]) for i in range(2)]
        adj_tb = [sb(f"adj_tb{i}", [P, H, N], BF16) for i in range(2)]
        adj_tf = sb("adj_tf", [P, H, N])
        x_t = sb("x_t", [D + 1, N])
        x_d = [sb(f"x_d{i}", [D + 1, N]) for i in range(2)]
        x_u = sb("x_u", [D + 1, N])
        c_val = sb("c_val", [P, NG * GS])
        c_sq = [sb(f"c_sq{i}", [P, H, 2 * D]) for i in range(2)]
        a_tok = [sb(f"a_tok{i}", [P, H, D]) for i in range(2)]
        table = sb("table", [P, NG, PAT])
        tab_t = sb("tab_t", [P, NT * P])
        tab_r = sb("tab_r", [P, NT * P])
        tab_p = sb("tab_p", [P, PARTS, NT * P], BF16)
        sel = [sb(f"sel{i}", [KR, GT, NT * P], BF16) for i in range(2)]
        onehot = [sb(f"onehot{i}", [KR, GT * N], BF16) for i in range(2)]
        ext = sb("ext", [P, GT * N])
        ext_r = sb("ext_r", [P, N])
        sums = sb("sums", [P, H, 2 * D + 1])
        deg_m = sb("deg_m", [P, H])
        rdeg = sb("rdeg", [P, H])
        rho = sb("rho", [P, H])
        mq = sb("mq", [P, H, 2 * D])
        m_sq = sb("m_sq", [P, H, D])
        var = sb("var", [P, H, D])
        var_c = sb("var_c", [P, H, D])
        rho_a = sb("rho_a", [P, H, D])
        m_s = sb("m_s", [P, H, 2 * D])
        ms_t = [sb(f"ms_t{i}", [P, N]) for i in range(2)]

        deg_1 = sb("deg_1", [P, T])
        log_deg = sb("log_deg", [P, T])
        log_c = sb("log_c", [P, T])
        log_r = sb("log_r", [P, T])
        amp = sb("amp", [P, T])
        att = sb("att", [P, T])
        u_att = sb("u_att", [P, TB, D])
        y = sb("y", [P, TB, D])
        y_c = sb("y_c", [P, TB, D])
        y_sq = sb("y_sq", [P, TB, D])
        h0 = sb("h0", [P, TB, D])
        st = sb("st", [P, 5, TB])
        n_new = adj_in[1][:].rearrange("p h (t d) -> p (h t) d", d=D)
        y_out = adj_in[0][:].rearrange("p h (t d) -> p (h t) d", d=D)
        h_n = adj_tf[:].rearrange("p h (t d) -> p (h t) d", d=D)
        mh = table[:].rearrange("p g c -> p (g c)")[:, 0:TB * P]
        m1_t = tab_t[0:D + 1, 0:TB * P]
        m2 = ext[:, 0:TB * D].rearrange("p (t d) -> p t d", d=D)
        m2_r = ext[:, TB * D:2 * TB * D].rearrange("p (t d) -> p t d", d=D)
        rz = tab_r[:, 0:TB * 2 * D].rearrange("p (t d) -> p t d", d=2 * D)
        m2_p = [sb(f"m2_p{i}", [P, TB, D], BF16) for i in range(PARTS)]
        n_arg = sb("n_arg", [P, TB, D])

        main_ps = [ctx.enter_context(nc.psum_tensor(f"main_ps{i}", [P, 1024], F32)) for i in range(2)]
        pool_ps = [ctx.enter_context(nc.psum_tensor(f"pool_ps{i}", [P, 1024], F32)) for i in range(2)]

        consts_in = sem("consts_in")
        x_ld = [sem(f"x_ld{i}") for i in range(2)]
        adj_ld = [sem(f"adj_ld{i}") for i in range(2)]
        sel_ld = [sem(f"sel_ld{i}") for i in range(2)]
        out_st = sem("out_st")
        v_pre = sem("v_pre")
        g_pre = sem("g_pre")
        t_pre = sem("t_pre")
        a_pre = sem("a_pre")
        filled = sem("filled")
        emptied = sem("emptied")
        c_ready = sem("c_ready")
        selected = sem("selected")
        folded = sem("folded")
        ext_done = sem("ext_done")
        tabled = sem("tabled")
        rdeg_s = sem("rdeg_s")
        stat = sem("stat")
        std_s = sem("std_s")
        split = sem("split")
        adj_kept = sem("adj_kept")
        x_kept = sem("x_kept")
        xu_s = sem("xu_s")
        STATS, SPLITS = 8, 4
        ZD = GT * PARTS * 16

        p_pe, p_act, p_dve, p_pool = sem("p_pe"), sem("p_act"), sem("p_dve"), sem("p_pool")
        ones_s = sem("ones_s")
        p_sc = sem("p_sc")
        G_PRE = 5
        NP_PE, NP_ACT, NP_DVE, NP_POOL = 5, 9, 20, 10

        block = ctx.enter_context(nc.Block())
        N_CONSTS = 16 * (1 + 6 + 15 + 6 + 4)
        post_rows = w_post.rearrange("(k e) d -> e k d", e=D)
        row = lambda v: v.rearrange("(a d) -> a d", a=1)

        @block.sync
        def _(sp):
            sp.dma_start(x_tok[0][:], x[0].rearrange("(h p) d -> p h d", p=P)).then_inc(x_ld[0], 16)
            sp.dma_start(x_tok[1][:], x[1].rearrange("(h p) d -> p h d", p=P)).then_inc(x_ld[1], 16)
            sp.dma_start(adj_in[0][:], adj[0].rearrange("(h p) m -> p h m", p=P)).then_inc(adj_ld[0], 16)
            sp.dma_start(ident[:], ident_c).then_inc(consts_in, 16)
            sp.dma_start(wc_pm[:, 0:D], w_pre[D:2 * D, :]).then_inc(consts_in, 16)
            sp.dma_start(w_tok[0:D, 0:D], w_pre[D:2 * D, :]).then_inc(consts_in, 16)
            sp.dma_start(w_tok[0:D, D:2 * D], w_pre[0:D, :]).then_inc(consts_in, 16)
            sp.wait_ge(v_pre, 1)
            sp.dma_start(w_tok[D:D + 1, D:2 * D], row(b_pre)).then_inc(consts_in, 16)
            sp.dma_start(mbias[:], mbias_c).then_inc(consts_in, 16)
            sp.dma_start(match[:], match_c).then_inc(consts_in, 16)
            for s in range(3):
                c = slice(s * D, (s + 1) * D)
                sp.dma_start(w_ext[0:D, c], post_rows[:, 2 + 4 * s, :]).then_inc(consts_in, 16)
                sp.dma_start(w_ext[D:P, c], post_rows[:, 3 + 4 * s, :]).then_inc(consts_in, 16)
                sp.dma_start(w_sum[:, c], post_rows[:, 3 + 4 * s, :]).then_inc(consts_in, 16)
                sp.dma_start(w_ms[0:D, c], post_rows[:, 1 + 4 * s, :]).then_inc(consts_in, 16)
                sp.dma_start(w_ms[D:P, c], post_rows[:, 4 + 4 * s, :]).then_inc(consts_in, 16)
            sp.dma_start(w_x[0:D, 0:D], post_rows[:, 0, :]).then_inc(consts_in, 16)
            sp.dma_start(w_x[D:D + 1, 0:D], row(b_post)).then_inc(consts_in, 16)
            sp.dma_start(w1_s[D:P, :], w1).then_inc(consts_in, 16)
            sp.dma_start(b1_s[:], b1.rearrange("(d a) -> d a", a=1)).then_inc(consts_in, 16)
            sp.dma_start(w2_s[0:D, :], w2).then_inc(consts_in, 16)
            sp.dma_start(w2_s[D:D + 1, :], row(b2)).then_inc(consts_in, 16)
            sp.dma_start(gru_raw[:, 0], w_ih.rearrange("(c p) d -> p c d", c=2)).then_inc(consts_in, 16)
            sp.dma_start(gru_raw[:, 1], w_hh.rearrange("(c p) d -> p c d", c=2)).then_inc(consts_in, 16)
            sp.dma_start(b_raw[:, 0, :], row(b_ih)).then_inc(consts_in, 16)
            sp.dma_start(b_raw[:, 1, :], row(b_hh)).then_inc(consts_in, 16)

            def lay_table(j, b, first=False):
                sp.wait_ge(split, (j * 2 + b + 1) * SPLITS)
                sp.nop(nofuse=True)
                if not first:
                    sp.wait_ge(selected, (j * 2 + b - 1) * NT)
                    sp.nop(nofuse=True)
                for q in range(GT):
                    for part in range(PARTS):
                        sp.dma_start(sel[b][PAT * part:PAT * (part + 1), q, :],
                                     tab_p[PAT * q:PAT * (q + 1), part, :]).then_inc(sel_ld[b], 16)

            def load_adj(g, b):
                sp.wait_ge(adj_kept, g - 1)
                sp.nop(nofuse=True)
                sp.dma_start(adj_in[b][:], adj[bass.ds(g, 1)].rearrange("a (h p) m -> p (a h) m", p=P)
                             ).then_inc(adj_ld[b], 16)

            def load_x(g, b):
                sp.wait_ge(x_kept, g - 1)
                sp.nop(nofuse=True)
                sp.dma_start(x_tok[b][:], x[bass.ds(g, 1)].rearrange("a (h p) d -> p (a h) d", p=P)
                             ).then_inc(x_ld[b], 16)

            for b in range(2):
                lay_table(0, b, first=True)
                load_adj(b + 1, 1 - b)
                load_x(b + 2, b)
            with sp.Fori(1, B // 2 - 1) as j:
                for b in range(2):
                    lay_table(j, b)
                    load_adj(j * 2 + (b + 1), 1 - b)
                    load_x(j * 2 + (b + 2), b)
            lay_table(B // 2 - 1, 0)
            load_adj(B - 1, 1)
            lay_table(B // 2 - 1, 1)

            tiles = out.rearrange("g (h p) d -> p (g h) d", p=P)
            def batch(i):
                sp.wait_ge(p_dve, i * NP_DVE + NP_DVE)
                sp.nop(nofuse=True)
                sp.dma_start(tiles[:, bass.ds(i * TB, TB), :], y_out).then_inc(out_st, 16)

            batch(0)
            with sp.Fori(1, B // QB) as i:
                batch(i)
            sp.wait_ge(out_st, 16 * (B // QB))

        @block.tensor
        def _(pe):
            def slot_free(k):
                if not (isinstance(k, int) and k < 2):
                    pe.wait_ge(emptied, k - 1)

            def adj_transpose(b, loads, k, s):
                pe.wait_ge(adj_ld[b], loads * 16)
                slot_free(k)
                for half in range(H):
                    for nh in range(H):
                        o = pool_ps[s][:, half * N + nh * P:half * N + (nh + 1) * P]
                        i = pe.transpose(o, adj_in[b][:, nh, half * P:(half + 1) * P], ident[:])
                        if half == H - 1 and nh == H - 1:
                            i.then_inc(filled, 1)

            def neighbour_sums(b, k, s, k_at):
                pe.wait_ge(emptied, k_at + 1)
                slot_free(k)
                for nh in range(H):
                    r = slice(nh * P, (nh + 1) * P)
                    for half in range(H):
                        pe.matmul(pool_ps[s][:, nh * 512:nh * 512 + 2 * D], adj_tf[:, half, r],
                                  c_sq[b][:, half, :], start=(half == 0), stop=(half == H - 1))
                    for half in range(H):
                        i = pe.matmul(pool_ps[s][:, nh * 512 + 2 * D:nh * 512 + 2 * D + 1],
                                      adj_tb[b][:, half, r], ones_col[:], start=(half == 0), stop=(half == H - 1))
                i.then_inc(filled, 1)

            def ms_transpose(g, k, s):
                pe.wait_ge(stat, g * STATS + 7)
                pe.wait_ge(std_s, g + 1)
                slot_free(k)
                for nh in range(H):
                    i = pe.transpose(pool_ps[s][:, nh * P:(nh + 1) * P], m_s[:, nh, :], ident[:])
                i.then_inc(filled, 1)

            def x_transpose(b, loads, k, s):
                pe.wait_ge(x_ld[b], loads * 16)
                slot_free(k)
                pe.nop(nofuse=True)
                for nh in range(H):
                    i = pe.transpose(pool_ps[s][0:D, nh * P:(nh + 1) * P], x_tok[b][:, nh, :], ident[:])
                i.then_inc(filled, 1)

            def values(k, s, k_xt):
                pe.wait_ge(emptied, k_xt + 1)
                slot_free(k)
                pe.matmul(pool_ps[s][:, 0:N], wc_pm[:], x_t[0:D, :], start=True, stop=True)
                for nh in range(H):
                    i = pe.matmul(pool_ps[s][:, 512 + nh * 2 * D:512 + (nh + 1) * 2 * D],
                                  x_t[:, nh * P:(nh + 1) * P], w_tok[:], start=True, stop=True)
                i.then_inc(filled, 1)

            def table_transpose(g, k, s, t0, t1):
                pe.wait_ge(tabled, g * GS + GS)
                slot_free(k)
                for t in range(t0, t1):
                    i = pe.transpose(pool_ps[s][:, (t - t0) * P:(t - t0 + 1) * P],
                                     table[:, GT * t:GT * (t + 1), :].rearrange("p g c -> p (g c)"), ident[:])
                i.then_inc(filled, 1)

            def match_tile(b, t, k, s):
                slot_free(k)
                for q in range(GT):
                    mine = [(i, half) for i, (g, half) in enumerate(BLOCKS) if g == GT * t + q]
                    for n, (i, half) in enumerate(mine):
                        last = pe.matmul(pool_ps[s][0:KR, q * N:(q + 1) * N], match[:, i, :],
                                         adj_tb[b][:, half, :], start=(n == 0), stop=(n == len(mine) - 1))
                last.then_inc(filled, 1)

            def select_tile(j, b, t, k_m):
                if t == 0:
                    pe.wait_ge(sel_ld[b], (j + 1) * ZD)
                pe.wait_ge(emptied, k_m + 1)
                if not (isinstance(j, int) and j == 0 and b == 0 and t < 2):
                    pe.wait_ge(folded, (j * 2 + b) * NT + (t - 1))
                s = (b + t) % 2
                for q in range(GT):
                    i = pe.matmul(main_ps[s][:, q * N:(q + 1) * N], sel[b][:, q, t * P:(t + 1) * P],
                                  onehot[s][:, q * N:(q + 1) * N], start=True, stop=True)
                i.then_inc(selected, 1)

            def post(g, b, k, s):
                pe.wait_ge(ext_done, g * 2 + 2)
                pe.wait_ge(xu_s, g + 1)
                slot_free(k)
                for nh in range(H):
                    o = pool_ps[s][:, nh * 512:nh * 512 + 3 * D]
                    r = slice(nh * P, (nh + 1) * P)
                    pe.matmul(o, ext_r[:, r], w_ext[:], start=True, stop=False)
                    pe.matmul(o, ms_t[b][:, r], w_ms[:], start=False, stop=False)
                    i = pe.matmul(o, x_u[:, r], w_x[:], start=False, stop=True)
                i.then_inc(filled, 1)

            def iteration(j, b):
                order, where = pool_order(j, b)
                g = j * 2 + b
                for t in range(NT):
                    for name, arg, k, s in order[t]:
                        if name == "M":
                            match_tile(b, arg, k, s)
                        elif name == "M0":
                            match_tile(1 - b, 0, k, s)
                        elif name == "AT":
                            adj_transpose(1 - b, j + (b + 1) // 2 + 1, k, s)
                        elif name == "SQ":
                            neighbour_sums(1 - b, k, s, where[("AT", 0)])
                        elif name == "MST":
                            ms_transpose(g + 1, k, s)
                        elif name == "XT":
                            x_transpose(b, j + 2, k, s)
                        elif name == "V":
                            values(k, s, where[("XT", 0)])
                        elif name == "TPA":
                            table_transpose(g + 2, k, s, 0, TA)
                        elif name == "TPB":
                            table_transpose(g + 2, k, s, TA, NT)
                        elif name == "U":
                            post(g - 1, 1 - b, k, s)
                    select_tile(j, b, t, where[("M", t)] if t else pool_base(j, b) - 1)

            pe.wait_ge(consts_in, N_CONSTS)
            pe.wait_ge(v_pre, 3)
            pe.wait_ge(g_pre, G_PRE)
            pe.transpose(pool_ps[0][0:D, 0:D + 1], w_tok[:, D:2 * D], ident[0:D + 1, 0:D + 1])
            for i in range(2):
                for c in range(2):
                    last = pe.transpose(pool_ps[1][0:D, i * 512 + c * 96:i * 512 + (c + 1) * 96],
                                        gru_raw[:, i, c, :], ident[0:96, 0:96])
            last.then_inc(t_pre, 1)
            pe.wait_ge(a_pre, 1)
            pe.matmul(main_ps[0][0:D + 1, 0:3 * D], wa_t[:], w_sum[:], start=True, stop=True).then_inc(t_pre, 1)
            pe.wait_ge(v_pre, 4)

            for g in range(2):
                x_transpose(g, 1, 4 * g, 0)
                values(4 * g + 1, 1, 4 * g)
                table_transpose(g, 4 * g + 2, 0, 0, TA)
                table_transpose(g, 4 * g + 3, 1, TA, NT)
            adj_transpose(0, 1, 8, 0)
            neighbour_sums(0, 9, 1, 8)
            ms_transpose(0, 10, 0)
            match_tile(0, 0, 11, 1)
            iteration(0, 0)
            iteration(0, 1)
            with pe.Fori(1, B // 2 - 1) as j:
                iteration(j, 0)
                iteration(j, 1)
            iteration(B // 2 - 1, 0)
            iteration(B // 2 - 1, 1)
            post(B - 1, 1, POOL_STEPS - 1, (POOL_STEPS - 1) % 2)

            pe.wait_ge(emptied, POOL_STEPS)
            pe.wait_ge(ones_s, 1)
            pe.wait_ge(adj_kept, B)
            def batch(i):
                pe.wait_ge(p_dve, i * NP_DVE + 9)
                pe.nop(nofuse=True)
                for t in range(TB):
                    last = pe.transpose(pool_ps[0][0:D, t * P:(t + 1) * P], h0[:, t, :], ident[:])
                last.then_inc(p_pe, 1)
                pe.wait_ge(p_act, i * NP_ACT + 2)
                pe.nop(nofuse=True)
                for c in range(2):
                    last = pe.matmul(pool_ps[1][0:D, c * 512:(c + 1) * 512], w1_s[D:P, :],
                                     mh[D:P, c * 512:(c + 1) * 512], start=True, stop=True)
                last.then_inc(p_pe, 1)
                pe.wait_ge(p_act, i * NP_ACT + 3)
                for t in range(TB):
                    last = pe.matmul(main_ps[0][:, t * D:(t + 1) * D], m1_t[:, t * P:(t + 1) * P], w2_s[:],
                                     start=True, stop=True)
                last.then_inc(p_pe, 1)
                pe.wait_ge(p_pool, i * NP_POOL + 6)
                for q in range(QB):
                    n = 0
                    for half in range(H):
                        for part in range(PARTS):
                            last = pe.matmul(main_ps[1][0:D, q * N:(q + 1) * N], m2_p[part][:, q * H + half, :],
                                             adjt_all[:, bass.ds(i * QB + q, 1), half * N:(half + 1) * N]
                                             .rearrange("p a n -> p (a n)"),
                                             start=(n == 0), stop=(n == H * PARTS - 1))
                            n += 1
                last.then_inc(p_pe, 1)
                pe.wait_ge(p_act, i * NP_ACT + 5)
                for t in range(TB):
                    o = pool_ps[t // 4][:, (t % 4) * 4 * D:(t % 4 + 1) * 4 * D]
                    pe.matmul(o, mh[:, t * P:(t + 1) * P], w_gru[:], start=True, stop=False)
                    last = pe.matmul(o, ones_row[:], b_gru[:], start=False, stop=True)
                last.then_inc(p_pe, 1)

            batch(0)
            with pe.Fori(1, B // QB) as i:
                batch(i)

        @block.scalar
        def _(act):
            def copy(o, i):
                return act.activation(o, i, ACT.Copy)

            def ready(k):
                act.wait_ge(filled, k + 1)

            def adj_out(g, b, k, s):
                ready(k)
                copy(adj_tf[:].rearrange("p h n -> p (h n)"), pool_ps[s][:, 0:H * N])
                if not (isinstance(g, int) and g < 2):
                    act.wait_ge(adj_kept, g - 1)
                copy(adj_tb[b][:].rearrange("p h n -> p (h n)"), pool_ps[s][:, 0:H * N]).then_inc(emptied, 1)

            def sums_out(g, k, s):
                ready(k)
                act.wait_ge(stat, g * STATS)
                act.activation(sums[:], pool_ps[s][:].rearrange("p (h n) -> p h n", h=H)[:, :, 0:2 * D + 1],
                               ACT.Copy).then_inc(emptied, 1)

            def std_out(g):
                act.wait_ge(stat, g * STATS + 5)
                act.activation(m_s[:, :, D:2 * D], var_c[:], ACT.Sqrt, bias=eps_col[:]).then_inc(std_s, 1)

            def ms_out(b, k, s):
                ready(k)
                copy(ms_t[b][:], pool_ps[s][:, 0:N]).then_inc(emptied, 1)

            def x_out(g, k, s):
                ready(k)
                act.wait_ge(x_kept, g)
                copy(x_t[0:D, :], pool_ps[s][0:D, 0:N]).then_inc(emptied, 1)

            def values_out(g, b, k, s):
                ready(k)
                if not (isinstance(g, int) and g < 1):
                    act.wait_ge(tabled, g * GS)
                copy(c_val[:, 0:N], pool_ps[s][:, 0:N]).then_inc(c_ready, 1)
                tok = pool_ps[s][:, 512:1024].rearrange("p (h n) -> p h n", h=2)[:, :, :]
                tok = pool_ps[s][:, 512:512 + H * 2 * D].rearrange("p (h n) -> p h n", h=H)
                copy(c_sq[b][:, :, 0:D], tok[:, :, 0:D])
                act.activation(c_sq[b][:, :, D:2 * D], tok[:, :, 0:D], ACT.Square)
                copy(a_tok[b][:], tok[:, :, D:2 * D]).then_inc(emptied, 1)

            def table_out(g, k, s, t0, t1):
                ready(k)
                act.wait_ge(split, g * SPLITS)
                copy(tab_t[:, t0 * P:t1 * P], pool_ps[s][:, 0:(t1 - t0) * P]).then_inc(emptied, 1)

            def onehots(j, b, t, k, s):
                ready(k)
                if not (isinstance(j, int) and j == 0 and b == 0 and t < 2):
                    act.wait_ge(selected, (j * 2 + b) * NT + (t - 1))
                act.activation(onehot[(b + t) % 2][:], pool_ps[s][0:KR, :], ACT.Relu,
                               bias=mbias[:]).then_inc(emptied, 1)

            def post_out(g, k, s):
                ready(k)
                act.activation(u_all[:, bass.ds(g * H, H), :],
                               pool_ps[s][:].rearrange("p (h n) -> p h n", h=H)[:, :, 0:3 * D],
                               ACT.Copy).then_inc(emptied, 1)

            def iteration(j, b):
                order, where = pool_order(j, b)
                g = j * 2 + b
                for t in range(NT):
                    for name, arg, k, s in order[t]:
                        if name == "M":
                            onehots(j, b, arg, k, s)
                        elif name == "M0":
                            onehots(j, b, NT, k, s)
                        elif name == "AT":
                            adj_out(g + 1, 1 - b, k, s)
                        elif name == "SQ":
                            sums_out(g + 1, k, s)
                        elif name == "STD":
                            std_out(g + 1)
                        elif name == "MST":
                            ms_out(1 - b, k, s)
                        elif name == "XT":
                            x_out(g + 2, k, s)
                        elif name == "V":
                            values_out(g + 2, b, k, s)
                        elif name == "TPA":
                            table_out(g + 2, k, s, 0, TA)
                        elif name == "TPB":
                            table_out(g + 2, k, s, TA, NT)
                        elif name == "U":
                            post_out(g - 1, k, s)

            act.wait_ge(t_pre, 1)
            act.wait_ge(v_pre, 3)
            copy(wa_t[:], pool_ps[0][0:D, 0:D + 1])
            copy(w_gru[0:D, 0:3 * D], pool_ps[1][0:D, 0:3 * D])
            copy(w_gru[D:P, 0:2 * D], pool_ps[1][0:D, 512:512 + 2 * D])
            copy(w_gru[D:P, 3 * D:4 * D], pool_ps[1][0:D, 512 + 2 * D:512 + 3 * D]).then_inc(a_pre, 1)
            for g in range(2):
                x_out(g, 4 * g, 0)
                values_out(g, g, 4 * g + 1, 1)
                table_out(g, 4 * g + 2, 0, 0, TA)
                table_out(g, 4 * g + 3, 1, TA, NT)
            adj_out(0, 0, 8, 0)
            sums_out(0, 9, 1)
            std_out(0)
            ms_out(0, 10, 0)
            onehots(0, 0, 0, 11, 1)
            iteration(0, 0)
            iteration(0, 1)
            with act.Fori(1, B // 2 - 1) as j:
                iteration(j, 0)
                iteration(j, 1)
            iteration(B // 2 - 1, 0)
            iteration(B // 2 - 1, 1)
            post_out(B - 1, POOL_STEPS - 1, (POOL_STEPS - 1) % 2)

            act.wait_ge(p_sc, 1)
            act.activation(log_deg[:], deg_1[:], ACT.Ln).then_inc(p_sc, 1)
            def batch(i):
                act.wait_ge(p_dve, i * NP_DVE + 6)
                act.activation(y_sq[:], y_c[:], ACT.Square).then_inc(p_act, 1)
                act.wait_ge(p_pe, i * NP_PE + 1)
                copy(mh[D:P, :], pool_ps[0][0:D, :]).then_inc(p_act, 1)
                act.wait_ge(p_pe, i * NP_PE + 2)
                act.activation(m1_t[0:D, :], pool_ps[1][0:D, :], ACT.Relu, bias=b1_s[:]).then_inc(p_act, 1)
                act.wait_ge(p_pe, i * NP_PE + 3)
                act.activation(m2.rearrange("p t d -> p (t d)"), main_ps[0][:, 0:TB * D],
                               ACT.Relu).then_inc(p_act, 1)
                act.wait_ge(p_pe, i * NP_PE + 4)
                act.activation(mh[0:D, :], main_ps[1][0:D, :], ACT.Relu).then_inc(p_act, 1)
                act.wait_ge(p_pe, i * NP_PE + 5)
                for s in range(2):
                    act.activation(rz[:, s * 4:(s + 1) * 4, :],
                                   pool_ps[s][:].rearrange("p (t n) -> p t n", t=4)[:, :, 0:2 * D],
                                   ACT.Sigmoid).then_inc(p_act, 1)
                act.wait_ge(p_dve, i * NP_DVE + 13)
                act.activation(n_new, n_arg[:], ACT.Tanh).then_inc(p_act, 1)
                act.wait_ge(p_dve, i * NP_DVE + 17)
                act.activation(y_sq[:], y_c[:], ACT.Square).then_inc(p_act, 1)

            batch(0)
            with act.Fori(1, B // QB) as i:
                batch(i)

        @block.vector
        def _(dve):
            def fold(j, b, t):
                g = j * 2 + b
                dve.wait_ge(selected, g * NT + (t + 1))
                if t == 0:
                    dve.wait_ge(ext_done, g * 2)
                    dve.tensor_copy(ext[:], main_ps[b % 2][:]).then_inc(folded, 1)
                else:
                    dve.wait_ge(folded, g * NT + t)
                    dve.tensor_tensor(ext[:], main_ps[(b + t) % 2][:], ext[:], ALU.max).then_inc(folded, 1)

            def extrema(j, b):
                g = j * 2 + b
                dve.wait_ge(folded, g * NT + NT)
                if not (isinstance(j, int) and j == 0 and b == 0):
                    dve.wait_ge(emptied, u_done(j, b))
                dve.tensor_tensor(ext[:, 0:2 * N], ext[:, 0:2 * N], ext[:, 2 * N:4 * N], ALU.max).then_inc(ext_done, 1)
                dve.wait_ge(ext_done, g * 2 + 1)
                dve.tensor_tensor(ext_r[:], ext[:, 0:N], ext[:, N:2 * N], ALU.max).then_inc(ext_done, 1)

            def u_done(j, b):
                return pool_order(j, b)[1][("U", 0)] + 1

            def double(g):
                dve.wait_ge(c_ready, g + 1)
                for i in range(GS):
                    if i:
                        dve.wait_ge(tabled, g * GS + i)
                    h = 1 << i
                    v = c_val[:].rearrange("p (g i) -> p g i", i=GS)[:, :, i:i + 1].to_broadcast([P, NG, h])
                    dve.tensor_tensor(table[:, :, h:2 * h], table[:, :, 0:h], v, ALU.max).then_inc(tabled, 1)

            def reciprocal_deg(g, k):
                dve.wait_ge(emptied, k + 1)
                if not (isinstance(g, int) and g == 0):
                    dve.wait_ge(stat, g * STATS)
                dve.tensor_scalar(deg_m[:], sums[:, :, 2 * D:2 * D + 1].rearrange("p h a -> p (h a)"), 1.0, None,
                                  ALU.max).then_inc(rdeg_s, 1)
                dve.wait_ge(rdeg_s, g * 2 + 1)
                dve.reciprocal(rdeg[:], deg_m[:]).then_inc(rdeg_s, 1)

            def iteration(j, b):
                _, has_x, has_adj, _ = iteration_flags(j, b)
                for t in range(NT):
                    fold(j, b, t)
                    if t == 5 and has_x:
                        double(j * 2 + (b + 2))
                    if t == 7 and has_adj:
                        reciprocal_deg(j * 2 + (b + 1), pool_order(j, b)[1][("SQ", 0)])
                extrema(j, b)

            dve.memset(w_tok[D:D + 1, 0:D], 0.0)
            dve.memset(w_x[:], 0.0).then_inc(v_pre, 1)
            dve.memset(w_gru[:], 0.0).then_inc(v_pre, 1)
            dve.memset(c_val[:, N:], NEG)
            for rows in (x_t[D:D + 1, :], x_u[D:D + 1, :], ones_row[:], ones_col[:]):
                dve.memset(rows, 1.0)
            dve.memset(m_half[:], -0.5)
            dve.memset(eps_col[:], EPS)
            dve.memset(table[:, :, 0:1], NEG).then_inc(v_pre, 1)
            dve.wait_ge(v_pre, 3)
            dve.wait_ge(t_pre, 2)
            dve.wait_ge(g_pre, G_PRE)
            dve.tensor_tensor(w_x[:], main_ps[0][0:D + 1, 0:3 * D], w_x[:], ALU.add).then_inc(v_pre, 1)
            double(0)
            double(1)
            reciprocal_deg(0, 9)
            iteration(0, 0)
            iteration(0, 1)
            with dve.Fori(1, B // 2 - 1) as j:
                iteration(j, 0)
                iteration(j, 1)
            iteration(B // 2 - 1, 0)
            iteration(B // 2 - 1, 1)

            dve.wait_ge(stat, B * STATS)
            dve.tensor_scalar(deg_1[:], deg_all[:], 1.0, None, ALU.add).then_inc(p_sc, 1)
            dve.wait_ge(p_sc, 2)
            dve.tensor_scalar(amp[:], log_deg[:], 1.0 / AVG, None, ALU.mult)
            dve.tensor_scalar(log_c[:], log_deg[:], EPS, None, ALU.max).then_inc(p_sc, 1)
            dve.wait_ge(p_sc, 3)
            dve.reciprocal(log_r[:], log_c[:]).then_inc(p_sc, 1)
            dve.wait_ge(p_sc, 4)
            dve.tensor_scalar(att[:], log_r[:], AVG, None, ALU.mult).then_inc(p_sc, 1)
            dve.wait_ge(p_sc, 5)
            dve.wait_ge(split, B * SPLITS)
            dve.memset(m1_t[D:D + 1, :], 1.0).then_inc(ones_s, 1)
            dve.wait_ge(emptied, POOL_STEPS)

            def columns(c):
                return c.unsqueeze(2).to_broadcast([P, TB, D])

            def centre(base):
                dve.tensor_reduce(st[:, 0, :], y[:], AX_X, ALU.add).then_inc(p_dve, 1)
                dve.wait_ge(p_dve, base + 1)
                dve.tensor_scalar(st[:, 1, :], st[:, 0, :], 1.0 / D, None, ALU.mult).then_inc(p_dve, 1)
                dve.wait_ge(p_dve, base + 2)
                dve.tensor_tensor(y_c[:], y[:], columns(st[:, 1, :]), ALU.subtract).then_inc(p_dve, 1)

            def scale(base, rooted, o):
                dve.tensor_reduce(st[:, 2, :], y_sq[:], AX_X, ALU.add).then_inc(p_dve, 1)
                dve.wait_ge(p_dve, base + 1)
                dve.tensor_scalar(st[:, 3, :], st[:, 2, :], 1.0 / D, EPS, ALU.mult, ALU.add).then_inc(p_dve, 1)
                dve.wait_ge(p_pool, rooted)
                dve.tensor_tensor(o, y_c[:], columns(st[:, 4, :]), ALU.mult).then_inc(p_dve, 1)

            def batch(i):
                base = i * NP_DVE
                tiles_i = bass.ds(i * TB, TB)
                if not isinstance(i, int):
                    dve.wait_ge(p_dve, base)
                dve.tensor_tensor(y_c[:], u_all[:, tiles_i, D:2 * D], columns(amp[:, tiles_i]),
                                  ALU.mult).then_inc(p_dve, 1)
                dve.wait_ge(p_dve, base + 1)
                dve.tensor_tensor(y_sq[:], u_all[:, tiles_i, 0:D], y_c[:], ALU.add).then_inc(p_dve, 1)
                dve.wait_ge(p_dve, base + 2)
                dve.wait_ge(p_pool, i * NP_POOL + 1)
                dve.tensor_tensor(y[:], y_sq[:], u_att[:], ALU.add).then_inc(p_dve, 1)
                dve.wait_ge(p_dve, base + 3)
                centre(base + 3)
                dve.wait_ge(p_act, i * NP_ACT + 1)
                scale(base + 6, i * NP_POOL + 2, h0[:])
                for s in range(2):
                    gates = pool_ps[s][:].rearrange("p (t n) -> p t n", t=4)
                    ts_ = slice(4 * s, 4 * s + 4)
                    dve.wait_ge(p_act, i * NP_ACT + 7)
                    dve.tensor_tensor(y_c[:, ts_, :], gates[:, :, 3 * D:4 * D], rz[:, ts_, 0:D],
                                      ALU.mult).then_inc(p_dve, 1)
                for s in range(2):
                    gates = pool_ps[s][:].rearrange("p (t n) -> p t n", t=4)
                    ts_ = slice(4 * s, 4 * s + 4)
                    dve.wait_ge(p_dve, base + 10 + s)
                    dve.tensor_tensor(n_arg[:, ts_, :], gates[:, :, 2 * D:3 * D], y_c[:, ts_, :],
                                      ALU.add).then_inc(p_dve, 1)
                dve.wait_ge(p_pool, i * NP_POOL + 9)
                dve.tensor_tensor(y[:], u_att[:], h_n, ALU.add).then_inc(p_dve, 1)
                dve.wait_ge(p_dve, base + 14)
                centre(base + 14)
                dve.wait_ge(p_act, i * NP_ACT + 9)
                if not isinstance(i, int):
                    dve.wait_ge(out_st, i * 16)
                scale(base + 17, i * NP_POOL + 10, y_out)

            batch(0)
            with dve.Fori(1, B // QB) as i:
                batch(i)

        @block.gpsimd
        def _(pool):
            def keep_adj(g, b, k):
                pool.wait_ge(emptied, k + 1)
                pool.nop(nofuse=True)
                pool.tensor_copy(adjt_all[:, bass.ds(g, 1), :].rearrange("p a n -> p (a n)"),
                                 adj_tb[b][:].rearrange("p h n -> p (h n)")).then_inc(adj_kept, 1)

            def keep_x(b, k, laid=None):
                if laid is not None:
                    pool.wait_ge(xu_s, laid)
                pool.wait_ge(emptied, k + 1)
                pool.nop(nofuse=True)
                pool.tensor_copy(x_d[b][:], x_t[:]).then_inc(x_kept, 1)

            def lay_x(b, k):
                if k is not None:
                    pool.wait_ge(emptied, k + 1)
                pool.nop(nofuse=True)
                pool.tensor_copy(x_u[:], x_d[b][:]).then_inc(xu_s, 1)

            def statistics(g, b):
                base = g * STATS
                pool.wait_ge(rdeg_s, g * 2 + 2)
                r = rdeg[:].unsqueeze(2).to_broadcast([P, H, 2 * D])
                deg = sums[:, :, 2 * D:2 * D + 1].rearrange("p h a -> p (h a)")
                pool.tensor_tensor(mq[:], sums[:, :, 0:2 * D], r, ALU.mult).then_inc(stat, 1)
                pool.tensor_tensor(rho[:], deg, rdeg[:], ALU.mult).then_inc(stat, 1)
                pool.wait_ge(stat, base + 1)
                pool.tensor_tensor(m_sq[:], mq[:, :, 0:D], mq[:, :, 0:D], ALU.mult).then_inc(stat, 1)
                pool.wait_ge(stat, base + 3)
                pool.tensor_tensor(var[:], mq[:, :, D:2 * D], m_sq[:], ALU.subtract).then_inc(stat, 1)
                pool.wait_ge(stat, base + 4)
                pool.nop(nofuse=True)
                pool.tensor_scalar(var_c[:], var[:], 0.0, None, ALU.max).then_inc(stat, 1)
                pool.tensor_tensor(rho_a[:], a_tok[b][:], rho[:].unsqueeze(2).to_broadcast([P, H, D]),
                                   ALU.mult).then_inc(stat, 1)
                pool.wait_ge(stat, base + 6)
                pool.tensor_tensor(m_s[:, :, 0:D], rho_a[:], mq[:, :, 0:D], ALU.add).then_inc(stat, 1)
                pool.tensor_copy(deg_all[:, bass.ds(g * H, H)], deg).then_inc(stat, 1)

            def split_table(g, b, loads_before, k):
                base = g * SPLITS
                pool.wait_ge(emptied, k + 1)
                if loads_before is not None:
                    pool.wait_ge(sel_ld[1 - b], loads_before * ZD)
                pool.nop(nofuse=True)
                pool.tensor_copy(tab_p[:, 0, :], tab_t[:]).then_inc(split, 1)
                pool.wait_ge(split, base + 1)
                pool.tensor_tensor(tab_r[:], tab_t[:], tab_p[:, 0, :], ALU.subtract).then_inc(split, 1)
                pool.wait_ge(split, base + 2)
                pool.nop(nofuse=True)
                pool.tensor_copy(tab_p[:, 1, :], tab_r[:]).then_inc(split, 1)
                pool.wait_ge(split, base + 3)
                pool.tensor_tensor(tab_p[:, 2, :], tab_r[:], tab_p[:, 1, :], ALU.subtract).then_inc(split, 1)

            def iteration(j, b):
                _, where = pool_order(j, b)
                has_u, has_x, has_adj, _ = iteration_flags(j, b)
                g = j * 2 + b
                lay_x(b, where[("U", 0)] if has_u else None)
                if has_adj:
                    keep_adj(g + 1, 1 - b, where[("AT", 0)])
                if has_x:
                    keep_x(b, where[("XT", 0)], g + 1)
                if has_adj:
                    statistics(g + 1, 1 - b)
                if has_x:
                    split_table(g + 2, b, j + b + 1, where[("TPB", 0)])

            pool.wait_ge(consts_in, N_CONSTS)
            pool.tensor_scalar(wc_pm[:, D:2 * D], wc_pm[:, 0:D], -1.0, None, ALU.mult).then_inc(g_pre, 1)
            pool.tensor_tensor(w_sum[:], w_sum[:], w_ext[0:D, :], ALU.add).then_inc(g_pre, 1)
            pool.tensor_tensor(w_x[0:D, 0:D], w_x[0:D, 0:D], ident[0:D, 0:D], ALU.add).then_inc(g_pre, 1)
            pool.wait_ge(g_pre, 3)
            pool.tensor_scalar(w_ext[D:P, :], w_ext[D:P, :], -1.0, None, ALU.mult).then_inc(g_pre, 1)
            pool.wait_ge(g_pre, 4)
            pool.tensor_tensor(b_gru[:, 0:2 * D], b_raw[:, 0, 0:2 * D], b_raw[:, 1, 0:2 * D], ALU.add)
            pool.tensor_copy(b_gru[:, 2 * D:3 * D], b_raw[:, 0, 2 * D:3 * D])
            pool.tensor_copy(b_gru[:, 3 * D:4 * D], b_raw[:, 1, 2 * D:3 * D]).then_inc(g_pre, 1)
            pool.wait_ge(g_pre, G_PRE)
            for g in range(2):
                keep_x(g, 4 * g)
                split_table(g, g, 1 if g else None, 4 * g + 3)
            keep_adj(0, 0, 8)
            statistics(0, 0)
            iteration(0, 0)
            iteration(0, 1)
            with pool.Fori(1, B // 2 - 1) as j:
                iteration(j, 0)
                iteration(j, 1)
            iteration(B // 2 - 1, 0)
            iteration(B // 2 - 1, 1)

            pool.wait_ge(p_sc, 5)
            pool.wait_ge(emptied, POOL_STEPS)
            def batch(i):
                base = i * NP_POOL
                tiles_i = bass.ds(i * TB, TB)
                if not isinstance(i, int):
                    pool.wait_ge(p_dve, i * NP_DVE)
                pool.tensor_tensor(u_att[:], u_all[:, tiles_i, 2 * D:3 * D],
                                   att[:, tiles_i].unsqueeze(2).to_broadcast([P, TB, D]),
                                   ALU.mult).then_inc(p_pool, 1)
                pool.wait_ge(p_dve, i * NP_DVE + 8)
                pool.tensor_tensor(st[:, 4, :], st[:, 3, :], m_half[:], ALU.pow).then_inc(p_pool, 1)
                pool.wait_ge(p_act, i * NP_ACT + 4)
                pool.nop(nofuse=True)
                pool.tensor_copy(m2_p[0][:], m2).then_inc(p_pool, 1)
                pool.wait_ge(p_pool, base + 3)
                pool.tensor_tensor(m2_r, m2, m2_p[0][:], ALU.subtract).then_inc(p_pool, 1)
                pool.wait_ge(p_pool, base + 4)
                pool.nop(nofuse=True)
                pool.tensor_copy(m2_p[1][:], m2_r).then_inc(p_pool, 1)
                pool.wait_ge(p_pool, base + 5)
                pool.tensor_tensor(m2_p[2][:], m2_r, m2_p[1][:], ALU.subtract).then_inc(p_pool, 1)
                pool.wait_ge(p_act, i * NP_ACT + 8)
                pool.tensor_tensor(y_sq[:], h0[:], n_new, ALU.subtract).then_inc(p_pool, 1)
                pool.tensor_tensor(h_n, h0[:], n_new, ALU.add).then_inc(p_pool, 1)
                pool.wait_ge(p_pool, base + 7)
                pool.tensor_tensor(u_att[:], y_sq[:], rz[:, :, D:2 * D], ALU.mult).then_inc(p_pool, 1)
                pool.wait_ge(p_dve, i * NP_DVE + 19)
                pool.tensor_tensor(st[:, 4, :], st[:, 3, :], m_half[:], ALU.pow).then_inc(p_pool, 1)

            batch(0)
            with pool.Fori(1, B // QB) as i:
                batch(i)

def kernel(x, adj, L0_gnn_W_pre, L0_gnn_b_pre, L0_gnn_W_post, L0_gnn_b_post, L1_gnn_W1, L1_gnn_b1,
           L1_gnn_W2, L1_gnn_b2, L1_gnn_W_ih, L1_gnn_b_ih, L1_gnn_W_hh, L1_gnn_b_hh):
    import ml_dtypes
    import concourse.bacc as bacc
    from concourse.bass_utils import run_bass_kernel_spmd

    given = [("x", x), ("adj", adj), ("w_pre", L0_gnn_W_pre), ("b_pre", L0_gnn_b_pre),
             ("w_post", L0_gnn_W_post), ("b_post", L0_gnn_b_post), ("w1", L1_gnn_W1), ("b1", L1_gnn_b1),
             ("w2", L1_gnn_W2), ("b2", L1_gnn_b2), ("w_ih", L1_gnn_W_ih), ("b_ih", L1_gnn_b_ih),
             ("w_hh", L1_gnn_W_hh), ("b_hh", L1_gnn_b_hh)]
    match_c, mbias_c = match_constants()
    constants = [("ident", np.eye(P, dtype=np.float32)), ("match", match_c.astype(ml_dtypes.bfloat16)),
                 ("mbias", mbias_c)]
    nc = bacc.Bacc("TRN2", target_bir_lowering=False, num_devices=1)
    arrays, args = {}, []
    for name, a in given + constants:
        a = np.ascontiguousarray(a)
        arrays[f"in_{name}"] = a
        args.append(nc.dram_tensor(f"in_{name}", a.shape, mybir.dt.from_np(a.dtype), kind="ExternalInput").ap())
    out = nc.dram_tensor("out", (B, N, D), F32, kind="ExternalOutput").ap()
    build(nc, *args, out)
    r = run_bass_kernel_spmd(nc, [arrays], core_ids=[0])
    return r.results[0]["out"]
```

```python
from contextlib import ExitStack

import numpy as np

import concourse.bass as bass
from concourse import mybir
from concourse.alu_op_type import AluOpType as ALU

F32 = mybir.dt.float32
BF16 = mybir.dt.bfloat16
ACT = mybir.ActivationFunctionType
AX_X = mybir.AxisListType.X

B, N, D = 32, 256, 64
P = 128
H = N // P
T = B * H
GS = 5
PAT = 1 << GS
PARTS = 3
KR = PARTS * PAT
GT = 4
NT = 13
NG = NT * GT
TA = 8
NEG = -1.0e9
EPS = 1e-5
AVG = 4.86
NPAIR = B // 2
TB = 2 * H


def match_blocks():
    blocks = []
    for g in range(NG):
        for half in range(H):
            if any(half * P <= m < (half + 1) * P for m in range(GS * g, min(GS * g + GS, N))):
                blocks.append((g, half))
    return blocks


BLOCKS = match_blocks()


def match_constants():
    w = np.zeros((P, len(BLOCKS), KR), np.float32)
    for i, (g, half) in enumerate(BLOCKS):
        for j in range(GS):
            m = GS * g + j - half * P
            if 0 <= m < P and GS * g + j < N:
                for r in range(KR):
                    w[m, i, r] = 1.0 if (r % PAT) >> j & 1 else -1.0
    bias = np.array([[1.0 - bin(r % PAT).count("1")] for r in range(KR)], np.float32)
    return w, bias


SPAN = 2 * NT
BANK, POOL_BANKS = 512, 4
POOL_STEPS = {
    ("M", 0, 0): -0.953, ("M", 0, 1): 0.314, ("M", 0, 2): 1.306, ("M", 0, 3): 2.427, ("M", 0, 4): 3.171,
    ("M", 0, 5): 4.260, ("M", 0, 6): 5.342, ("M", 0, 7): 5.729, ("M", 0, 8): 7.181, ("M", 0, 9): 7.609,
    ("M", 0, 10): 8.680, ("M", 0, 11): 10.224, ("M", 0, 12): 10.915, ("M", 1, 0): 11.541, ("M", 1, 1): 12.842,
    ("M", 1, 2): 14.315, ("M", 1, 3): 15.299, ("M", 1, 4): 16.322, ("M", 1, 5): 17.260, ("M", 1, 6): 18.297,
    ("M", 1, 7): 18.935, ("M", 1, 8): 20.329, ("M", 1, 9): 20.761, ("M", 1, 10): 21.611, ("M", 1, 11): 23.142,
    ("M", 1, 12): 24.326,
    ("XT", 0, 0): -24.388, ("XT", 1, 0): -11.302,
    ("V", 0, 0): -23.048, ("V", 1, 0): -9.618,
    ("TPA", 0, 0): -15.725, ("TPA", 1, 0): -3.590,
    ("TPB", 0, 0): -14.332, ("TPB", 1, 0): -0.803,
    ("AT", 0, 0): -11.648, ("AT", 1, 0): 1.123,
    ("SQ", 0, 0): -4.770, ("SQ", 1, 0): 6.975,
    ("MST", 0, 0): 2.595, ("MST", 1, 0): 15.595,
    ("U", 0, 0): 15.354, ("U", 1, 0): 28.354,
    ("HT", 0, 0): 43.177,
    ("M1", 0, 0): 46.464,
    ("M2", 0, 0): 52.712,
    ("MSG", 0, 0): 55.199,
    ("GA", 0, 0): 58.090,
    ("GB", 0, 0): 59.532,
}
ACT_STEPS = {
    ("STD", 0, 0): 0.313, ("STD", 1, 0): 14.641,
    ("NEW", 0, 0): 63.607,
    ("LOG", 0, 0): 28.097,
    ("SQO", 0, 0): 71.029,
    ("SQH", 0, 0): 31.602,
}
VECTOR_STEPS = {
    ("FOLD", 0, 0): 0.500, ("FOLD", 0, 1): 1.500, ("FOLD", 0, 2): 2.500, ("FOLD", 0, 3): 3.500,
    ("FOLD", 0, 4): 4.500, ("FOLD", 0, 5): 5.500, ("FOLD", 0, 6): 6.500, ("FOLD", 0, 7): 7.500,
    ("FOLD", 0, 8): 8.500, ("FOLD", 0, 9): 9.500, ("FOLD", 0, 10): 10.500, ("FOLD", 0, 11): 11.500,
    ("FOLD", 0, 12): 12.500, ("FOLD", 1, 0): 13.500, ("FOLD", 1, 1): 14.500, ("FOLD", 1, 2): 15.500,
    ("FOLD", 1, 3): 16.500, ("FOLD", 1, 4): 17.500, ("FOLD", 1, 5): 18.500, ("FOLD", 1, 6): 19.500,
    ("FOLD", 1, 7): 20.500, ("FOLD", 1, 8): 21.500, ("FOLD", 1, 9): 22.500, ("FOLD", 1, 10): 23.500,
    ("FOLD", 1, 11): 24.500, ("FOLD", 1, 12): 25.500,
    ("TABLE", 0, 0): -22.712, ("TABLE", 0, 1): -22.555, ("TABLE", 0, 2): -21.277, ("TABLE", 0, 3): -18.547,
    ("TABLE", 0, 4): -17.847, ("TABLE", 1, 0): -9.026, ("TABLE", 1, 1): -8.663, ("TABLE", 1, 2): -7.993,
    ("TABLE", 1, 3): -7.179, ("TABLE", 1, 4): -6.332,
    ("RDEG", 0, 0): -3.208, ("RDEG", 1, 0): 10.080,
    ("EXT", 0, 0): 12.575, ("EXT", 1, 0): 25.575,
    ("FIRST", 0, 0): 28.175, ("FIRST", 0, 1): 28.303, ("FIRST", 0, 2): 28.815, ("FIRST", 0, 3): 29.315,
    ("FIRST", 0, 4): 30.170, ("FIRST", 0, 5): 32.064, ("FIRST", 0, 6): 40.066,
    ("SECOND", 0, 0): 61.255, ("SECOND", 0, 1): 62.588, ("SECOND", 0, 2): 66.878, ("SECOND", 0, 3): 67.601,
    ("SECOND", 0, 4): 72.131, ("SECOND", 0, 5): 77.595,
}
GPSIMD_STEPS = {
    ("SPLIT", 0, 0): -12.415, ("SPLIT", 0, 1): -11.532, ("SPLIT", 0, 2): -5.277, ("SPLIT", 0, 3): -5.184,
    ("SPLIT", 1, 0): -0.159, ("SPLIT", 1, 1): 3.601, ("SPLIT", 1, 2): 6.315, ("SPLIT", 1, 3): 6.904,
    ("STAT", 0, 0): -0.375, ("STAT", 1, 0): 11.031,
    ("WIDEN", 0, 0): -10.972, ("WIDEN", 1, 0): 1.993,
    ("CELL", 0, 0): 63.361,
    ("ROOT2", 0, 0): 73.630,
    ("ATT", 0, 0): 27.461,
    ("ROOT1", 0, 0): 36.846,
    ("M2S", 0, 0): 53.417,
}
SYNC_STEPS = {
    ("LOAD_X", 0, 0): -43.111, ("LOAD_X", 1, 0): -29.566,
    ("KEEP_X", 0, 0): -32.272, ("KEEP_X", 1, 0): -13.151,
    ("LOAD_ADJ", 0, 0): -28.269, ("LOAD_ADJ", 1, 0): -15.058,
    ("KEEP_ADJ", 0, 0): -25.044, ("KEEP_ADJ", 1, 0): -12.356,
    ("LAY_TABLE", 0, 0): -20.554, ("LAY_TABLE", 0, 1): -18.952, ("LAY_TABLE", 0, 2): -17.320,
    ("LAY_TABLE", 1, 0): -10.367, ("LAY_TABLE", 1, 1): -9.273, ("LAY_TABLE", 1, 2): -4.320,
    ("LAY_X", 0, 0): -11.591, ("LAY_X", 1, 0): 4.133,
    ("STORE", 0, 0): 67.759,
}
PE_STEPS = POOL_STEPS | {("SELECT", b, t): b * NT + t + 0.5 for b in range(2) for t in range(NT)}
LOOP = range(3, NPAIR - 1)
PAIRS = range(-2, NPAIR + 2)


class Pair:

    def __init__(self, j, lag=0):
        self.j, self.lag = j, lag

    def __call__(self, per, plus=0):
        return self.j * per + (self.lag * per + plus)


class Count:

    def __init__(self, j, per, plus):
        self.j, self.per, self.plus = j, per, plus

    def __add__(self, n):
        return Count(self.j, self.per, self.plus + n)


def later(a, b):
    return max(a, b) if isinstance(a, int) else max(a, b, key=lambda c: c.plus)


def through(step):
    return step + 1 if isinstance(step, int) else step.j * step.per + (step.plus + 1)


def exists(j, lag):
    return not isinstance(j, int) or 0 <= j + lag < NPAIR


def due(place, j):
    full = sorted(place, key=lambda n: place[n] % SPAN)
    return [(n, Pair(j, -int(place[n] // SPAN))) for n in full if exists(j, -int(place[n] // SPAN))]


def pool_base(j):
    return sum(len(due(POOL_STEPS, i)) for i in range(PAIRS[0], j))


def pool_step(q, name, b=0, t=0):
    n = (name, b, t)
    shift = q.lag + int(POOL_STEPS[n] // SPAN)
    if isinstance(q.j, int):
        return pool_base(q.j + shift) + [m for m, _ in due(POOL_STEPS, q.j + shift)].index(n)
    at = [m for m, _ in due(POOL_STEPS, q.j)].index(n)
    per = len(POOL_STEPS)
    return Count(q.j, per, pool_base(LOOP[0]) + (shift - LOOP[0]) * per + at)


def pool_banks(j):
    if not isinstance(j, int):
        return pool_banks(LOOP[1])
    had, base, got = {}, 0, []
    for i in range(max(PAIRS[0], j - 2), j + 1):
        bank = 0
        for n, _ in due(POOL_STEPS, i):
            size = 2 if n[0] in ("M", "TPA", "TPB") else 1
            if bank + size > POOL_BANKS:
                bank = 0
            last = max(had.get(bank + c, -POOL_BANKS) for c in range(size))
            if i == j:
                got.append((bank, base - last))
            for c in range(size):
                had[bank + c] = base
            bank = (bank + size) % POOL_BANKS
            base += 1
    return got


def pool_place(q, n):
    names = [m for m, _ in due(POOL_STEPS, q.j)]
    bank, back = pool_banks(q.j)[names.index(n)]
    k = pool_step(q, *n)
    return k, bank * BANK, k + -back


def some(n):
    return not isinstance(n, int) or n > 0


def build(nc, x, adj, w_pre, b_pre, w_post, b_post, w1, b1, w2, b2, w_ih, b_ih, w_hh, b_hh,
          ident_c, match_c, mbias_c, out):
    ctx = ExitStack()
    with ctx:
        def sb(name, shape, dt=F32):
            return ctx.enter_context(nc.sbuf_tensor(name, shape, dt))

        def sem(name):
            return ctx.enter_context(nc.semaphore(name))

        ident = sb("ident", [P, P])
        match = sb("match", [P, len(BLOCKS), KR], BF16)
        mbias = sb("mbias", [KR, 1])
        eps_col = sb("eps_col", [P, 1])
        m_half = sb("m_half", [P, TB])
        ones_col = sb("ones_col", [P, 1], BF16)
        wc_pm = sb("wc_pm", [D, 2 * D])
        w_tok = sb("w_tok", [D + 1, 2 * D])
        w_ext = sb("w_ext", [P, 3 * D])
        w_ms = sb("w_ms", [P, 3 * D])
        w_sum = sb("w_sum", [D, 3 * D])
        w_x = sb("w_x", [D + 1, 3 * D])
        wa_t = sb("wa_t", [D, D + 1])
        w1_s = sb("w1_s", [P, D])
        b1_s = sb("b1_s", [D, 1])
        w2_s = sb("w2_s", [D + 1, D])
        w_gru = sb("w_gru", [P, 4 * D])
        gru_raw = sb("gru_raw", [96, 2, 2, D])
        b_gru = sb("b_gru", [1, 4 * D])
        b_res = sb("b_res", [1, 2, 4 * D])
        b_row = sb("b_row", [1, PARTS, 4 * D], BF16)
        b_parts = sb("b_parts", [PARTS, 4 * D], BF16)
        ones_p = sb("ones_p", [PARTS, P], BF16)
        zero = sb("zero", [P, 1])
        one = sb("one", [P, 1])
        b_raw = sb("b_raw", [1, 2, 3 * D])

        adjt_all = sb("adjt_all", [P, B, H * N], BF16)
        deg_all = sb("deg_all", [P, T])

        adj_in = [sb(f"adj_in{i}", [P, H, N]) for i in range(2)]
        x_tok = [sb(f"x_tok{i}", [P, H, D]) for i in range(2)]
        adj_tb = [sb(f"adj_tb{i}", [P, H, N], BF16) for i in range(2)]
        adj_tf = sb("adj_tf", [P, H, N])
        x_t = sb("x_t", [D + 1, N])
        x_d = [sb(f"x_d{i}", [D + 1, N]) for i in range(2)]
        x_u = sb("x_u", [D + 1, N])
        c_val = sb("c_val", [P, NG * GS])
        c_sq = [sb(f"c_sq{i}", [P, H, 2 * D]) for i in range(2)]
        a_tok = [sb(f"a_tok{i}", [P, H, D]) for i in range(2)]
        table = sb("table", [P, NG, PAT])
        tab_t = sb("tab_t", [P, NT * P])
        tab_r = sb("tab_r", [P, NT * P])
        tab_p = sb("tab_p", [P, PARTS, NT * P], BF16)
        sel = [sb(f"sel{i}", [KR, GT, NT * P], BF16) for i in range(2)]
        onehot = [sb(f"onehot{i}", [KR, GT * N], BF16) for i in range(2)]
        ext = sb("ext", [P, GT * N])
        ext_r = sb("ext_r", [P, N])
        sums = sb("sums", [P, H, 2 * D + 1])
        deg_m = sb("deg_m", [P, H])
        rdeg = sb("rdeg", [P, H])
        rho = sb("rho", [P, H])
        mq = sb("mq", [P, H, 2 * D])
        m_sq = sb("m_sq", [P, H, D])
        var = sb("var", [P, H, D])
        var_c = sb("var_c", [P, H, D])
        rho_a = sb("rho_a", [P, H, D])
        m_s = sb("m_s", [P, H, 2 * D])
        ms_t = [sb(f"ms_t{i}", [P, N]) for i in range(2)]

        u_p = sb("u_p", [P, TB, 3 * D])
        log_deg = sb("log_deg", [P, TB])
        amp = sb("amp", [P, TB])
        log_c = sb("log_c", [P, TB])
        att = sb("att", [P, TB])
        u_amp = sb("u_amp", [P, TB, D])
        u_att = sb("u_att", [P, TB, D])
        y_part = sb("y_part", [P, TB, D])
        norm = [{n: sb(f"{n}{i}", [P, TB, D]) for n in ("y", "centred", "squares")} for i in range(2)]
        stats = [sb(f"stats{i}", [P, 4, TB]) for i in range(2)]
        h = sb("h", [P, TB, D])
        mh = sb("mh", [P, TB * P])
        m1_t = sb("m1_t", [D + 1, TB * P])
        m2 = sb("m2", [P, TB, D])
        m2_r = sb("m2_r", [P, TB, D])
        m2_p = [sb(f"m2_p{i}", [P, TB, D], BF16) for i in range(PARTS)]
        rz = sb("rz", [P, TB, 2 * D])
        n_parts = sb("n_parts", [P, TB, 2 * D])
        r_h = sb("r_h", [P, TB, D])
        n_arg = sb("n_arg", [P, TB, D])
        n_new = sb("n_new", [P, TB, D])
        h_minus_n = sb("h_minus_n", [P, TB, D])
        h_plus_n = sb("h_plus_n", [P, TB, D])
        z_part = sb("z_part", [P, TB, D])
        y_out = sb("y_out", [P, TB, D])

        main_ps = [ctx.enter_context(nc.psum_tensor(f"main_ps{i}", [P, 1024], F32)) for i in range(2)]
        pool_ps = ctx.enter_context(nc.psum_tensor("pool_ps", [P, POOL_BANKS * BANK], F32))

        first_in = sem("first_in")
        match_in = sem("match_in")
        weights_in = sem("weights_in")
        x_ld = [sem(f"x_ld{i}") for i in range(2)]
        adj_ld = [sem(f"adj_ld{i}") for i in range(2)]
        sel_ld = [sem(f"sel_ld{i}") for i in range(2)]
        out_st = sem("out_st")
        v_pre = sem("v_pre")
        t_pre = sem("t_pre")
        a_pre = sem("a_pre")
        filled = sem("filled")
        emptied = sem("emptied")
        c_ready = sem("c_ready")
        selected = sem("selected")
        folded = sem("folded")
        ext_done = sem("ext_done")
        tabled = sem("tabled")
        rdeg_s = sem("rdeg_s")
        stat = sem("stat")
        std_s = sem("std_s")
        split = sem("split")
        adj_kept = [sem(f"adj_kept{i}") for i in range(2)]
        x_kept = sem("x_kept")
        xu_s = sem("xu_s")
        widened = sem("widened")
        STATS, SPLITS = 8, 4
        ZD = GT * PARTS * 16

        READY, BIAS_ROWS, W_READY = 4, 13, 14
        FIRST, WEIGHTS = 5 * 16, 15 * 16

        v_h = sem("v_h")
        v_o = sem("v_o")
        g_h = sem("g_h")
        g_o = sem("g_o")
        a_h = sem("a_h")
        a_o = sem("a_o")
        bias_ld = sem("bias_ld")
        V_H, V_O, G_H, G_O, A_H, A_O = 11, 8, 6, 4, 2, 2

        block = ctx.enter_context(nc.Block())
        post_rows = w_post.rearrange("(k e) d -> e k d", e=D)
        row = lambda v: v.rearrange("(a d) -> a d", a=1)

        @block.sync
        def _(sp):
            sp.dma_start(wc_pm[:, 0:D], w_pre[D:2 * D, :]).then_inc(first_in, 16)
            sp.dma_start(x_tok[0][:], x[0].rearrange("(h p) d -> p h d", p=P)).then_inc(x_ld[0], 16)
            sp.dma_start(ident[:], ident_c).then_inc(first_in, 16)
            sp.dma_start(w_tok[0:D, 0:D], w_pre[D:2 * D, :]).then_inc(first_in, 16)
            sp.dma_start(w_tok[0:D, D:2 * D], w_pre[0:D, :]).then_inc(first_in, 16)
            sp.wait_ge(v_pre, 1)
            sp.dma_start(w_tok[D:D + 1, D:2 * D], row(b_pre)).then_inc(first_in, 16)
            sp.dma_start(adj_in[0][:], adj[0].rearrange("(h p) m -> p h m", p=P)).then_inc(adj_ld[0], 16)
            sp.dma_start(x_tok[1][:], x[1].rearrange("(h p) d -> p h d", p=P)).then_inc(x_ld[1], 16)
            sp.dma_start(mbias[:], mbias_c).then_inc(match_in, 16)
            sp.dma_start(match[:], match_c).then_inc(match_in, 16)
            scalers = lambda w: w.rearrange("p (s d) -> p s d", s=3)
            for rows, k in ((w_ext[0:D, :], 2), (w_ext[D:P, :], 3), (w_sum[:], 3), (w_ms[0:D, :], 1),
                            (w_ms[D:P, :], 4)):
                sp.dma_start(scalers(rows), post_rows[:, k:k + 9:4, :]).then_inc(weights_in, 16)
            sp.dma_start(w_x[0:D, 0:D], post_rows[:, 0, :]).then_inc(weights_in, 16)
            sp.dma_start(w_x[D:D + 1, 0:D], row(b_post)).then_inc(weights_in, 16)
            sp.dma_start(w1_s[D:P, :], w1).then_inc(weights_in, 16)
            sp.dma_start(b1_s[:], b1.rearrange("(d a) -> d a", a=1)).then_inc(weights_in, 16)
            sp.dma_start(w2_s[0:D, :], w2).then_inc(weights_in, 16)
            sp.dma_start(w2_s[D:D + 1, :], row(b2)).then_inc(weights_in, 16)
            sp.dma_start(gru_raw[:, 0], w_ih.rearrange("(c p) d -> p c d", c=2)).then_inc(weights_in, 16)
            sp.dma_start(gru_raw[:, 1], w_hh.rearrange("(c p) d -> p c d", c=2)).then_inc(weights_in, 16)
            sp.dma_start(b_raw[:, 0, :], row(b_ih)).then_inc(weights_in, 16)
            sp.dma_start(b_raw[:, 1, :], row(b_hh)).then_inc(weights_in, 16)
            sp.dma_start(adj_in[1][:], adj[1].rearrange("(h p) m -> p h m", p=P)).then_inc(adj_ld[1], 16)

            def lay_table(q, b, part):
                sp.wait_ge(split, q(2 * SPLITS, b * SPLITS + (1, 3, 4)[part]))
                sp.nop(nofuse=True)
                if part == 0:
                    if some(n := q(2 * NT, (b - 1) * NT)):
                        sp.wait_ge(selected, n)
                    sp.nop(nofuse=True)
                for k in range(GT):
                    sp.dma_start(sel[b][PAT * part:PAT * (part + 1), k, :],
                                 tab_p[PAT * k:PAT * (k + 1), part, :]).then_inc(sel_ld[b], 16)

            def keep_adj(q, b):
                sp.wait_ge(emptied, through(pool_step(q, "AT", b)))
                sp.nop(nofuse=True)
                sp.dma_start(adjt_all[:, bass.ds(q(2, b), 1), :].rearrange("p a n -> p (a n)"),
                             adj_tb[b][:].rearrange("p h n -> p (h n)")).then_inc(adj_kept[b], 16)

            def keep_x(q, b):
                sp.wait_ge(emptied, through(pool_step(q, "XT", b)))
                sp.nop(nofuse=True)
                sp.dma_start(x_d[b][:], x_t[:]).then_inc(x_kept, 16)

            def lay_x(q, b):
                if not (b == 0 and isinstance(q.j, int) and q.j + q.lag == 0):
                    before = pool_step(q, "U", 0) if b else pool_step(Pair(q.j, q.lag - 1), "U", 1)
                    sp.wait_ge(emptied, through(before))
                    sp.nop(nofuse=True)
                sp.wait_ge(x_kept, q(32, b * 16 + 16))
                sp.nop(nofuse=True)
                sp.dma_start(x_u[:], x_d[b][:]).then_inc(xu_s, 16)
                sp.wait_ge(xu_s, q(32, b * 16 + 16))
                sp.nop(nofuse=True)

            def load_adj(q, b):
                if not (isinstance(q.j, int) and q.j + q.lag == 0):
                    sp.dma_start(adj_in[b][:], adj[bass.ds(q(2, b), 1)].rearrange("a (h p) m -> p (a h) m", p=P)
                                 ).then_inc(adj_ld[b], 16)

            def load_x(q, b):
                if not (isinstance(q.j, int) and q.j + q.lag == 0):
                    sp.dma_start(x_tok[b][:], x[bass.ds(q(2, b), 1)].rearrange("a (h p) d -> p (a h) d", p=P)
                                 ).then_inc(x_ld[b], 16)

            tiles = out.rearrange("g (h p) d -> p (g h) d", p=P)

            def store(q):
                sp.wait_ge(v_o, q(V_O, V_O))
                sp.nop(nofuse=True)
                sp.dma_start(tiles[:, bass.ds(q(TB), TB), :], y_out[:]).then_inc(out_st, 16)

            def pair(j):
                for (name, b, part), q in due(SYNC_STEPS, j):
                    if name == "LOAD_X":
                        load_x(q, b)
                    elif name == "LOAD_ADJ":
                        load_adj(q, b)
                    elif name == "KEEP_X":
                        keep_x(q, b)
                    elif name == "KEEP_ADJ":
                        keep_adj(q, b)
                    elif name == "LAY_TABLE":
                        lay_table(q, b, part)
                    elif name == "LAY_X":
                        lay_x(q, b)
                    elif name == "STORE":
                        store(q)

            for j in range(PAIRS[0], 1):
                pair(j)
            sp.wait_ge(v_pre, BIAS_ROWS)
            for part in range(PARTS):
                sp.dma_start(b_parts[part:part + 1, :], b_row[:, part, :]).then_inc(bias_ld, 16)
            for j in range(1, LOOP[0]):
                pair(j)
            with sp.Fori(LOOP[0], NPAIR - 2) as j:
                pair(j)
            for j in range(NPAIR - 2, PAIRS[-1] + 1):
                pair(j)
            sp.wait_ge(out_st, 16 * NPAIR)

        @block.tensor
        def _(pe):
            def adj_transpose(q, b, c, past):
                if some(n := through(past)):
                    pe.wait_ge(emptied, n)
                pe.wait_ge(adj_ld[b], q(16, 16))
                for half in range(H):
                    for nh in range(H):
                        o = pool_ps[:, c + half * N + nh * P:c + half * N + (nh + 1) * P]
                        i = pe.transpose(o, adj_in[b][:, nh, half * P:(half + 1) * P], ident[:])
                        if half == H - 1 and nh == H - 1:
                            i.then_inc(filled, 1)

            def neighbour_sums(q, b, c, past):
                if some(n := through(past)):
                    pe.wait_ge(emptied, n)
                pe.wait_ge(widened, q(2, b + 1))
                for nh in range(H):
                    r = slice(nh * P, (nh + 1) * P)
                    for half in range(H):
                        pe.matmul(pool_ps[:, c + nh * N:c + nh * N + 2 * D], adj_tf[:, half, r],
                                  c_sq[b][:, half, :], start=(half == 0), stop=(half == H - 1))
                    for half in range(H):
                        i = pe.matmul(pool_ps[:, c + nh * N + 2 * D:c + nh * N + 2 * D + 1],
                                      adj_tb[b][:, half, r], ones_col[:], start=(half == 0), stop=(half == H - 1))
                i.then_inc(filled, 1)

            def ms_transpose(q, b, c, past):
                if some(n := through(past)):
                    pe.wait_ge(emptied, n)
                pe.wait_ge(stat, q(2 * STATS, b * STATS + 7))
                pe.wait_ge(std_s, q(2, b + 1))
                for nh in range(H):
                    i = pe.transpose(pool_ps[:, c + nh * P:c + (nh + 1) * P], m_s[:, nh, :], ident[:])
                i.then_inc(filled, 1)

            def x_transpose(q, b, c, past):
                if some(n := through(past)):
                    pe.wait_ge(emptied, n)
                pe.wait_ge(x_ld[b], q(16, 16))
                pe.nop(nofuse=True)
                for nh in range(H):
                    i = pe.transpose(pool_ps[0:D, c + nh * P:c + (nh + 1) * P], x_tok[b][:, nh, :], ident[:])
                i.then_inc(filled, 1)

            def values(q, b, c, past):
                pe.wait_ge(emptied, through(later(past, pool_step(q, "XT", b))))
                pe.matmul(pool_ps[:, c:c + N], wc_pm[:], x_t[0:D, :], start=True, stop=True)
                for nh in range(H):
                    i = pe.matmul(pool_ps[:, c + N + nh * 2 * D:c + N + (nh + 1) * 2 * D],
                                  x_t[:, nh * P:(nh + 1) * P], w_tok[:], start=True, stop=True)
                i.then_inc(filled, 1)

            def table_transpose(q, b, c, past, t0, t1):
                if some(n := through(past)):
                    pe.wait_ge(emptied, n)
                pe.wait_ge(tabled, q(2 * GS, b * GS + GS))
                for t in range(t0, t1):
                    i = pe.transpose(pool_ps[:, c + (t - t0) * P:c + (t - t0 + 1) * P],
                                     table[:, GT * t:GT * (t + 1), :].rearrange("p g c -> p (g c)"), ident[:])
                i.then_inc(filled, 1)

            def match_tile(q, b, t, c, past):
                if b == 0 and t == 0 and isinstance(q.j, int) and q.j + q.lag == 0:
                    pe.wait_ge(match_in, 32)
                if some(n := through(past)):
                    pe.wait_ge(emptied, n)
                for u in range(GT):
                    mine = [(i, half) for i, (g, half) in enumerate(BLOCKS) if g == GT * t + u]
                    for n, (i, half) in enumerate(mine):
                        last = pe.matmul(pool_ps[0:KR, c + u * N:c + (u + 1) * N], match[:, i, :],
                                         adj_tb[b][:, half, :], start=(n == 0), stop=(n == len(mine) - 1))
                last.then_inc(filled, 1)

            def select_tile(q, b, t):
                if t == 0:
                    pe.wait_ge(sel_ld[b], q(ZD, ZD))
                if some(n := q(2 * NT, b * NT + t - 1)):
                    pe.wait_ge(folded, n)
                pe.wait_ge(emptied, through(pool_step(q, "M", b, t)))
                s = (b + t) % 2
                for u in range(GT):
                    i = pe.matmul(main_ps[s][:, u * N:(u + 1) * N], sel[b][:, u, t * P:(t + 1) * P],
                                  onehot[s][:, u * N:(u + 1) * N], start=True, stop=True)
                i.then_inc(selected, 1)

            def post(q, b, c, past):
                pe.wait_ge(emptied, through(later(past, pool_step(q, "MST", b))))
                pe.wait_ge(xu_s, q(32, b * 16 + 16))
                pe.wait_ge(ext_done, q(4, b * 2 + 2))
                for nh in range(H):
                    o = pool_ps[:, c + nh * N:c + nh * N + 3 * D]
                    r = slice(nh * P, (nh + 1) * P)
                    pe.matmul(o, ext_r[:, r], w_ext[:], start=True, stop=False)
                    pe.matmul(o, ms_t[b][:, r], w_ms[:], start=False, stop=False)
                    i = pe.matmul(o, x_u[:, r], w_x[:], start=False, stop=True)
                i.then_inc(filled, 1)

            def h_transpose(q, c, past):
                if some(n := through(past)):
                    pe.wait_ge(emptied, n)
                pe.wait_ge(v_h, q(V_H, V_H))
                pe.nop(nofuse=True)
                for t in range(TB):
                    i = pe.transpose(pool_ps[0:D, c + t * P:c + (t + 1) * P], h[:, t, :], ident[:])
                i.then_inc(filled, 1)

            def m1_product(q, c, past):
                pe.wait_ge(emptied, through(later(past, pool_step(q, "HT"))))
                pe.nop(nofuse=True)
                pe.matmul(pool_ps[0:D, c:c + TB * P], w1_s[D:P, :], mh[D:P, :], start=True, stop=True
                          ).then_inc(filled, 1)

            def m2_product(q, c, past):
                pe.wait_ge(emptied, through(later(past, pool_step(q, "M1"))))
                for t in range(TB):
                    i = pe.matmul(pool_ps[:, c + t * D:c + (t + 1) * D], m1_t[:, t * P:(t + 1) * P], w2_s[:],
                                  start=True, stop=True)
                i.then_inc(filled, 1)

            def message(q, c, past):
                if some(n := through(past)):
                    pe.wait_ge(emptied, n)
                pe.wait_ge(adj_kept[0], q(16, 16))
                pe.wait_ge(adj_kept[1], q(16, 16))
                pe.wait_ge(g_h, q(G_H, G_H))
                for b in range(2):
                    for half in range(H):
                        for part in range(PARTS):
                            i = pe.matmul(pool_ps[0:D, c + b * N:c + (b + 1) * N], m2_p[part][:, b * H + half, :],
                                          adjt_all[:, bass.ds(q(2, b), 1), half * N:(half + 1) * N]
                                          .rearrange("p a n -> p (a n)"),
                                          start=(half == 0 and part == 0), stop=(half == H - 1 and part == PARTS - 1))
                i.then_inc(filled, 1)

            def gates(q, c, past, t0):
                if isinstance(q.j, int) and q.j + q.lag == 0:
                    pe.wait_ge(bias_ld, PARTS * 16)
                pe.wait_ge(emptied, through(later(past, pool_step(q, "MSG"))))
                for t in range(2):
                    o = pool_ps[:, c + t * 4 * D:c + (t + 1) * 4 * D]
                    pe.matmul(o, mh[:, (t0 + t) * P:(t0 + t + 1) * P], w_gru[:], start=True, stop=False)
                    i = pe.matmul(o, ones_p[:], b_parts[:], start=False, stop=True)
                i.then_inc(filled, 1)

            def pair(j):
                for (name, b, t), q in due(PE_STEPS, j):
                    if name == "SELECT":
                        select_tile(q, b, t)
                        continue
                    _, c, past = pool_place(q, (name, b, t))
                    if name == "M":
                        match_tile(q, b, t, c, past)
                    elif name == "AT":
                        adj_transpose(q, b, c, past)
                    elif name == "SQ":
                        neighbour_sums(q, b, c, past)
                    elif name == "MST":
                        ms_transpose(q, b, c, past)
                    elif name == "XT":
                        x_transpose(q, b, c, past)
                    elif name == "V":
                        values(q, b, c, past)
                    elif name == "TPA":
                        table_transpose(q, b, c, past, 0, TA)
                    elif name == "TPB":
                        table_transpose(q, b, c, past, TA, NT)
                    elif name == "U":
                        post(q, b, c, past)
                    elif name == "HT":
                        h_transpose(q, c, past)
                    elif name == "M1":
                        m1_product(q, c, past)
                    elif name == "M2":
                        m2_product(q, c, past)
                    elif name == "MSG":
                        message(q, c, past)
                    elif name == "GA":
                        gates(q, c, past, 0)
                    elif name == "GB":
                        gates(q, c, past, 2)

            pe.wait_ge(v_pre, READY)
            pe.wait_ge(first_in, FIRST)
            for j in range(PAIRS[0], 0):
                pair(j)
            pe.wait_ge(weights_in, WEIGHTS)
            pe.transpose(main_ps[1][0:D, N:N + D + 1], w_tok[:, D:2 * D], ident[0:D + 1, 0:D + 1])
            for i in range(2):
                for c in range(2):
                    last = pe.transpose(main_ps[1][0:D, i * 512 + c * 96:i * 512 + (c + 1) * 96],
                                        gru_raw[:, i, c, :], ident[0:96, 0:96])
            last.then_inc(t_pre, 1)
            pe.wait_ge(a_pre, 1)
            pe.wait_ge(v_pre, READY + 1)
            pe.matmul(main_ps[0][0:D + 1, 0:3 * D], wa_t[:], w_sum[:], start=True, stop=True).then_inc(t_pre, 1)
            pe.wait_ge(v_pre, W_READY)
            for j in range(0, LOOP[0]):
                pair(j)
            with pe.Fori(LOOP[0], LOOP[-1] + 1) as j:
                pair(j)
            for j in range(LOOP[-1] + 1, PAIRS[-1] + 1):
                pair(j)

        @block.scalar
        def _(act):
            def copy(o, i):
                return act.activation(o, i, ACT.Copy)

            def adj_out(q, b, k, c):
                if some(n := q(16)):
                    act.wait_ge(adj_kept[b], n)
                act.wait_ge(filled, through(k))
                copy(adj_tb[b][:].rearrange("p h n -> p (h n)"), pool_ps[:, c:c + H * N]).then_inc(emptied, 1)

            def sums_out(q, b, k, c):
                if some(n := q(2 * STATS, b * STATS)):
                    act.wait_ge(stat, n)
                act.wait_ge(filled, through(k))
                act.activation(sums[:], pool_ps[:, c:c + H * N].rearrange("p (h n) -> p h n", h=H)[:, :, 0:2 * D + 1],
                               ACT.Copy).then_inc(emptied, 1)

            def std_out(q, b):
                act.wait_ge(stat, q(2 * STATS, b * STATS + 5))
                act.activation(m_s[:, :, D:2 * D], var_c[:], ACT.Sqrt, bias=eps_col[:]).then_inc(std_s, 1)

            def ms_out(b, k, c):
                act.wait_ge(filled, through(k))
                copy(ms_t[b][:], pool_ps[:, c:c + N]).then_inc(emptied, 1)

            def x_out(q, b, k, c):
                if some(n := q(32, b * 16)):
                    act.wait_ge(x_kept, n)
                act.wait_ge(filled, through(k))
                copy(x_t[0:D, :], pool_ps[0:D, c:c + N]).then_inc(emptied, 1)

            def values_out(q, b, k, c):
                if some(n := q(2 * GS, b * GS)):
                    act.wait_ge(tabled, n)
                act.wait_ge(filled, through(k))
                copy(c_val[:, 0:N], pool_ps[:, c:c + N]).then_inc(c_ready, 1)
                tok = pool_ps[:, c + N:c + N + H * 2 * D].rearrange("p (h n) -> p h n", h=H)
                copy(c_sq[b][:, :, 0:D], tok[:, :, 0:D])
                act.activation(c_sq[b][:, :, D:2 * D], tok[:, :, 0:D], ACT.Square)
                copy(a_tok[b][:], tok[:, :, D:2 * D]).then_inc(emptied, 1)

            def table_out(q, b, k, c, t0, t1):
                if some(n := q(2 * SPLITS, (b - 1) * SPLITS + 2)):
                    act.wait_ge(split, n)
                act.wait_ge(filled, through(k))
                copy(tab_t[:, t0 * P:t1 * P], pool_ps[:, c:c + (t1 - t0) * P]).then_inc(emptied, 1)

            def onehots(q, b, t, k, c):
                if some(n := q(2 * NT, b * NT + t - 1)):
                    act.wait_ge(selected, n)
                act.wait_ge(filled, through(k))
                act.activation(onehot[(b + t) % 2][:], pool_ps[0:KR, c:c + GT * N], ACT.Relu,
                               bias=mbias[:]).then_inc(emptied, 1)

            def post_out(q, b, k, c):
                if some(n := q(V_H, 6 - V_H)):
                    act.wait_ge(v_h, n)
                act.wait_ge(filled, through(k))
                act.activation(u_p[:, b * H:(b + 1) * H, :],
                               pool_ps[:, c:c + H * N].rearrange("p (h n) -> p h n", h=H)[:, :, 0:3 * D],
                               ACT.Copy).then_inc(emptied, 1)

            def h_out(k, c):
                act.wait_ge(filled, through(k))
                copy(mh[D:P, :], pool_ps[0:D, c:c + TB * P]).then_inc(emptied, 1)

            def m1_out(k, c):
                act.wait_ge(filled, through(k))
                act.activation(m1_t[0:D, :], pool_ps[0:D, c:c + TB * P], ACT.Relu, bias=b1_s[:]).then_inc(emptied, 1)

            def m2_out(k, c):
                act.wait_ge(filled, through(k))
                act.activation(m2[:].rearrange("p t d -> p (t d)"), pool_ps[:, c:c + TB * D],
                               ACT.Relu).then_inc(emptied, 1)

            def message_out(k, c):
                act.wait_ge(filled, through(k))
                act.activation(mh[0:D, :], pool_ps[0:D, c:c + TB * P], ACT.Relu).then_inc(emptied, 1)

            def gates_out(q, k, c, t0):
                if some(n := q(G_O, 3 - G_O)):
                    act.wait_ge(g_o, n)
                act.wait_ge(filled, through(k))
                g_ = pool_ps[:, c:c + 8 * D].rearrange("p (t n) -> p t n", t=2)
                act.activation(rz[:, t0:t0 + 2, :], g_[:, :, 0:2 * D], ACT.Sigmoid)
                act.activation(n_parts[:, t0:t0 + 2, :], g_[:, :, 2 * D:4 * D], ACT.Copy).then_inc(emptied, 1)

            def log_degree(q):
                act.wait_ge(stat, q(2 * STATS, 2 * STATS))
                if some(n := q(V_H, 3 - V_H)):
                    act.wait_ge(v_h, n)
                act.activation(log_deg[:], deg_all[:, bass.ds(q(TB), TB)], ACT.Ln, bias=one[:]).then_inc(a_h, 1)

            def squares_h(q):
                act.wait_ge(v_h, q(V_H, 8))
                act.activation(norm[0]["squares"][:], norm[0]["centred"][:], ACT.Square).then_inc(a_h, 1)

            def new_state(q):
                act.wait_ge(v_o, q(V_O, 2))
                act.activation(n_new[:], n_arg[:], ACT.Tanh).then_inc(a_o, 1)

            def squares_o(q):
                act.wait_ge(v_o, q(V_O, 5))
                act.activation(norm[1]["squares"][:], norm[1]["centred"][:], ACT.Square).then_inc(a_o, 1)

            def pair(j):
                for n, q in due(POOL_STEPS | ACT_STEPS, j):
                    name, b, t = n
                    if name == "STD":
                        std_out(q, b)
                    elif name == "LOG":
                        log_degree(q)
                    elif name == "SQH":
                        squares_h(q)
                    elif name == "NEW":
                        new_state(q)
                    elif name == "SQO":
                        squares_o(q)
                    if n in ACT_STEPS:
                        continue
                    k, c, _ = pool_place(q, n)
                    if name == "M":
                        onehots(q, b, t, k, c)
                    elif name == "AT":
                        adj_out(q, b, k, c)
                    elif name == "SQ":
                        sums_out(q, b, k, c)
                    elif name == "MST":
                        ms_out(b, k, c)
                    elif name == "XT":
                        x_out(q, b, k, c)
                    elif name == "V":
                        values_out(q, b, k, c)
                    elif name == "TPA":
                        table_out(q, b, k, c, 0, TA)
                    elif name == "TPB":
                        table_out(q, b, k, c, TA, NT)
                    elif name == "U":
                        post_out(q, b, k, c)
                    elif name == "HT":
                        h_out(k, c)
                    elif name == "M1":
                        m1_out(k, c)
                    elif name == "M2":
                        m2_out(k, c)
                    elif name == "MSG":
                        message_out(k, c)
                    elif name == "GA":
                        gates_out(q, k, c, 0)
                    elif name == "GB":
                        gates_out(q, k, c, 2)

            act.wait_ge(v_pre, READY)
            for j in range(PAIRS[0], 0):
                pair(j)
            act.wait_ge(t_pre, 1)
            copy(wa_t[:], main_ps[1][0:D, N:N + D + 1])
            copy(w_gru[0:D, 0:3 * D], main_ps[1][0:D, 0:3 * D])
            copy(w_gru[D:P, 0:2 * D], main_ps[1][0:D, 512:512 + 2 * D])
            copy(w_gru[D:P, 3 * D:4 * D], main_ps[1][0:D, 512 + 2 * D:512 + 3 * D]).then_inc(a_pre, 1)
            for j in range(0, LOOP[0]):
                pair(j)
            with act.Fori(LOOP[0], LOOP[-1] + 1) as j:
                pair(j)
            for j in range(LOOP[-1] + 1, PAIRS[-1] + 1):
                pair(j)

        @block.vector
        def _(dve):
            def fold(q, b, t):
                if t == 0:
                    if some(n := q(4, b * 2)):
                        dve.wait_ge(ext_done, n)
                    dve.wait_ge(selected, q(2 * NT, b * NT + t + 1))
                    dve.tensor_copy(ext[:], main_ps[b % 2][:]).then_inc(folded, 1)
                else:
                    if some(n := q(2 * NT, b * NT + t)):
                        dve.wait_ge(folded, n)
                    dve.wait_ge(selected, q(2 * NT, b * NT + t + 1))
                    dve.tensor_tensor(ext[:], main_ps[(b + t) % 2][:], ext[:], ALU.max).then_inc(folded, 1)

            def extrema(q, b):
                if not (b == 0 and isinstance(q.j, int) and q.j + q.lag == 0):
                    before = pool_step(q, "U", 0) if b else pool_step(Pair(q.j, q.lag - 1), "U", 1)
                    dve.wait_ge(emptied, through(before))
                dve.wait_ge(folded, q(2 * NT, b * NT + NT))
                dve.tensor_tensor(ext[:, 0:2 * N], ext[:, 0:2 * N], ext[:, 2 * N:4 * N], ALU.max).then_inc(ext_done, 1)
                dve.wait_ge(ext_done, q(4, b * 2 + 1))
                dve.tensor_tensor(ext_r[:], ext[:, 0:N], ext[:, N:2 * N], ALU.max).then_inc(ext_done, 1)

            def double(q, b, i):
                if i == 0:
                    dve.wait_ge(c_ready, q(2, b + 1))
                else:
                    dve.wait_ge(tabled, q(2 * GS, b * GS + i))
                n = 1 << i
                v = c_val[:].rearrange("p (g i) -> p g i", i=GS)[:, :, i:i + 1].to_broadcast([P, NG, n])
                dve.tensor_tensor(table[:, :, n:2 * n], table[:, :, 0:n], v, ALU.max).then_inc(tabled, 1)

            def reciprocal_deg(q, b):
                if some(n := q(2 * STATS, b * STATS)):
                    dve.wait_ge(stat, n)
                dve.wait_ge(emptied, through(pool_step(q, "SQ", b)))
                dve.tensor_scalar(deg_m[:], sums[:, :, 2 * D:2 * D + 1].rearrange("p h a -> p (h a)"), 1.0, None,
                                  ALU.max).then_inc(rdeg_s, 1)
                dve.wait_ge(rdeg_s, q(4, b * 2 + 1))
                dve.reciprocal(rdeg[:], deg_m[:]).then_inc(rdeg_s, 1)

            def columns(c):
                return c.unsqueeze(2).to_broadcast([P, TB, D])

            def centre(i, done, start, total):
                y, st = norm[i]["y"], stats[i]
                dve.wait_ge(done, start)
                dve.tensor_reduce(st[:, 0, :], y[:], AX_X, ALU.add).then_inc(done, 1)
                dve.wait_ge(done, total)
                dve.scalar_tensor_tensor(norm[i]["centred"][:], columns(st[:, 0, :]), -1.0 / D, y[:],
                                         ALU.mult, ALU.add).then_inc(done, 1)

            def variance(i, done, total):
                st = stats[i]
                dve.tensor_reduce(st[:, 1, :], norm[i]["squares"][:], AX_X, ALU.add).then_inc(done, 1)
                dve.wait_ge(done, total)
                dve.tensor_scalar(st[:, 2, :], st[:, 1, :], 1.0 / D, EPS, ALU.mult, ALU.add).then_inc(done, 1)

            def first_layer(q, step):
                if step == 0:
                    dve.wait_ge(a_h, q(A_H, 1))
                    dve.tensor_scalar(amp[:], log_deg[:], 1.0 / AVG, None, ALU.mult).then_inc(v_h, 1)
                    dve.tensor_scalar(log_c[:], log_deg[:], EPS, 1.0 / AVG, ALU.max, ALU.mult).then_inc(v_h, 1)
                    dve.wait_ge(v_h, q(V_H, 2))
                    dve.reciprocal(att[:], log_c[:]).then_inc(v_h, 1)
                elif step == 1:
                    dve.wait_ge(v_h, q(V_H, 1))
                    dve.wait_ge(emptied, through(pool_step(q, "U", 1)))
                    dve.tensor_tensor(u_amp[:], u_p[:, :, D:2 * D], columns(amp[:]), ALU.mult).then_inc(v_h, 1)
                elif step == 2:
                    dve.wait_ge(v_h, q(V_H, 4))
                    dve.tensor_tensor(y_part[:], u_p[:, :, 0:D], u_amp[:], ALU.add).then_inc(v_h, 1)
                elif step == 3:
                    dve.wait_ge(v_h, q(V_H, 5))
                    dve.wait_ge(g_h, q(G_H, 1))
                    dve.tensor_tensor(norm[0]["y"][:], y_part[:], u_att[:], ALU.add).then_inc(v_h, 1)
                elif step == 4:
                    centre(0, v_h, q(V_H, 6), q(V_H, 7))
                elif step == 5:
                    dve.wait_ge(a_h, q(A_H, 2))
                    variance(0, v_h, q(V_H, 9))
                elif step == 6:
                    if some(n := q(G_O, 3 - G_O)):
                        dve.wait_ge(g_o, n)
                    dve.wait_ge(g_h, q(G_H, 2))
                    dve.tensor_tensor(h[:], norm[0]["centred"][:], columns(stats[0][:, 3, :]),
                                      ALU.mult).then_inc(v_h, 1)

            def second_layer(q, step):
                if step == 0:
                    dve.wait_ge(emptied, through(pool_step(q, "GB")))
                    dve.tensor_tensor(r_h[:], n_parts[:, :, D:2 * D], rz[:, :, 0:D], ALU.mult).then_inc(v_o, 1)
                elif step == 1:
                    dve.wait_ge(v_o, q(V_O, 1))
                    dve.tensor_tensor(n_arg[:], n_parts[:, :, 0:D], r_h[:], ALU.add).then_inc(v_o, 1)
                elif step == 2:
                    dve.wait_ge(g_o, q(G_O, 3))
                    dve.tensor_tensor(norm[1]["y"][:], z_part[:], h_plus_n[:], ALU.add).then_inc(v_o, 1)
                elif step == 3:
                    centre(1, v_o, q(V_O, 3), q(V_O, 4))
                elif step == 4:
                    dve.wait_ge(a_o, q(A_O, 2))
                    variance(1, v_o, q(V_O, 6))
                elif step == 5:
                    if some(n := q(16)):
                        dve.wait_ge(out_st, n)
                    dve.wait_ge(g_o, q(G_O, 4))
                    dve.tensor_tensor(y_out[:], norm[1]["centred"][:], columns(stats[1][:, 3, :]),
                                      ALU.mult).then_inc(v_o, 1)

            def split_first_table():
                dve.wait_ge(emptied, through(pool_step(Pair(0), "TPB", 0)))
                dve.tensor_copy(tab_p[:, 0, :], tab_t[:]).then_inc(split, 1)
                dve.wait_ge(split, 1)
                dve.tensor_tensor(tab_r[:], tab_t[:], tab_p[:, 0, :], ALU.subtract).then_inc(split, 1)
                dve.wait_ge(split, 2)
                dve.tensor_copy(tab_p[:, 1, :], tab_r[:]).then_inc(split, 1)
                dve.wait_ge(split, 3)
                dve.tensor_tensor(tab_p[:, 2, :], tab_r[:], tab_p[:, 1, :], ALU.subtract).then_inc(split, 1)

            def pair(j):
                for (name, b, i), q in due(VECTOR_STEPS, j):
                    if name == "FOLD":
                        fold(q, b, i)
                    elif name == "EXT":
                        extrema(q, b)
                    elif name == "TABLE":
                        double(q, b, i)
                        if isinstance(j, int) and j == -1 and b == 0 and i == GS - 1:
                            split_first_table()
                    elif name == "RDEG":
                        reciprocal_deg(q, b)
                    elif name == "FIRST":
                        first_layer(q, i)
                    elif name == "SECOND":
                        second_layer(q, i)

            dve.memset(w_tok[D:D + 1, 0:D], 0.0)
            dve.memset(w_x[:], 0.0).then_inc(v_pre, 1)
            dve.memset(w_gru[:], 0.0).then_inc(v_pre, 1)
            dve.memset(c_val[:, N:], NEG)
            for rows in (x_t[D:D + 1, :], m1_t[D:D + 1, :], ones_col[:], ones_p[:], one[:]):
                dve.memset(rows, 1.0)
            dve.memset(m_half[:], -0.5)
            dve.memset(zero[:], 0.0)
            dve.memset(eps_col[:], EPS)
            dve.memset(table[:, :, 0:1], NEG).then_inc(v_pre, 1)
            dve.wait_ge(first_in, FIRST)
            dve.tensor_scalar(wc_pm[:, D:2 * D], wc_pm[:, 0:D], -1.0, None, ALU.mult).then_inc(v_pre, 1)
            dve.wait_ge(v_pre, READY)
            for j in range(PAIRS[0], 0):
                pair(j)
            dve.wait_ge(weights_in, WEIGHTS)
            dve.tensor_tensor(w_sum[:], w_sum[:], w_ext[0:D, :], ALU.add).then_inc(v_pre, 1)
            dve.tensor_tensor(w_x[0:D, 0:D], w_x[0:D, 0:D], ident[0:D, 0:D], ALU.add).then_inc(v_pre, 1)
            dve.tensor_scalar(w_ext[D:P, :], w_ext[D:P, :], -1.0, None, ALU.mult).then_inc(v_pre, 1)
            dve.tensor_tensor(b_gru[:, 0:2 * D], b_raw[:, 0, 0:2 * D], b_raw[:, 1, 0:2 * D], ALU.add)
            dve.tensor_copy(b_gru[:, 2 * D:3 * D], b_raw[:, 0, 2 * D:3 * D])
            dve.tensor_copy(b_gru[:, 3 * D:4 * D], b_raw[:, 1, 2 * D:3 * D]).then_inc(v_pre, 1)
            dve.wait_ge(v_pre, READY + 4)
            dve.tensor_copy(b_row[:, 0, :], b_gru[:]).then_inc(v_pre, 1)
            dve.wait_ge(v_pre, READY + 5)
            dve.tensor_tensor(b_res[:, 0, :], b_gru[:], b_row[:, 0, :], ALU.subtract).then_inc(v_pre, 1)
            dve.wait_ge(v_pre, READY + 6)
            dve.tensor_copy(b_row[:, 1, :], b_res[:, 0, :]).then_inc(v_pre, 1)
            dve.wait_ge(v_pre, READY + 7)
            dve.tensor_tensor(b_res[:, 1, :], b_res[:, 0, :], b_row[:, 1, :], ALU.subtract).then_inc(v_pre, 1)
            dve.wait_ge(v_pre, READY + 8)
            dve.tensor_copy(b_row[:, 2, :], b_res[:, 1, :]).then_inc(v_pre, 1)
            dve.wait_ge(t_pre, 2)
            dve.tensor_tensor(w_x[:], main_ps[0][0:D + 1, 0:3 * D], w_x[:], ALU.add).then_inc(v_pre, 1)
            for j in range(0, LOOP[0]):
                pair(j)
            with dve.Fori(LOOP[0], LOOP[-1] + 1) as j:
                pair(j)
            for j in range(LOOP[-1] + 1, PAIRS[-1] + 1):
                pair(j)

        @block.gpsimd
        def _(pool):
            def statistics(q, b):
                base = b * STATS
                pool.wait_ge(rdeg_s, q(4, b * 2 + 2))
                r = rdeg[:].unsqueeze(2).to_broadcast([P, H, 2 * D])
                deg = sums[:, :, 2 * D:2 * D + 1].rearrange("p h a -> p (h a)")
                pool.tensor_tensor(mq[:], sums[:, :, 0:2 * D], r, ALU.mult).then_inc(stat, 1)
                pool.tensor_tensor(rho[:], deg, rdeg[:], ALU.mult).then_inc(stat, 1)
                pool.wait_ge(stat, q(2 * STATS, base + 1))
                pool.tensor_tensor(m_sq[:], mq[:, :, 0:D], mq[:, :, 0:D], ALU.mult).then_inc(stat, 1)
                pool.wait_ge(stat, q(2 * STATS, base + 3))
                pool.tensor_tensor(var[:], mq[:, :, D:2 * D], m_sq[:], ALU.subtract).then_inc(stat, 1)
                pool.wait_ge(stat, q(2 * STATS, base + 4))
                pool.nop(nofuse=True)
                pool.tensor_scalar(var_c[:], var[:], 0.0, None, ALU.max).then_inc(stat, 1)
                pool.tensor_tensor(rho_a[:], a_tok[b][:], rho[:].unsqueeze(2).to_broadcast([P, H, D]),
                                   ALU.mult).then_inc(stat, 1)
                pool.wait_ge(stat, q(2 * STATS, base + 6))
                pool.tensor_tensor(m_s[:, :, 0:D], rho_a[:], mq[:, :, 0:D], ALU.add).then_inc(stat, 1)
                pool.tensor_tensor(deg_all[:, bass.ds(q(2 * H, b * H), H)], deg,
                                   zero[:].to_broadcast([P, H]), ALU.add).then_inc(stat, 1)

            def as_sum(o, i, z):
                return pool.tensor_tensor(o, i, z, ALU.add)

            def widen(q, b):
                pool.wait_ge(emptied, through(pool_step(q, "AT", b)))
                as_sum(adj_tf[:], adj_tb[b][:], zero[:].unsqueeze(2).to_broadcast([P, H, N])).then_inc(widened, 1)

            zero_row = zero[:].to_broadcast([P, NT * P])

            def split_table(q, b, step):
                done = q(2 * SPLITS, b * SPLITS + step)
                if step == 0:
                    if b == 1 and isinstance(q.j, int) and q.j + q.lag == 0:
                        pool.wait_ge(split, SPLITS)
                    if some(n := q(ZD, b * ZD)):
                        pool.wait_ge(sel_ld[1 - b], n)
                    pool.wait_ge(emptied, through(pool_step(q, "TPB", b)))
                    as_sum(tab_p[:, 0, :], tab_t[:], zero_row).then_inc(split, 1)
                elif step == 1:
                    pool.wait_ge(split, done)
                    pool.tensor_tensor(tab_r[:], tab_t[:], tab_p[:, 0, :], ALU.subtract).then_inc(split, 1)
                elif step == 2:
                    pool.wait_ge(split, done)
                    as_sum(tab_p[:, 1, :], tab_r[:], zero_row).then_inc(split, 1)
                elif step == 3:
                    pool.wait_ge(split, done)
                    pool.tensor_tensor(tab_p[:, 2, :], tab_r[:], tab_p[:, 1, :], ALU.subtract).then_inc(split, 1)

            def root(i, done):
                pool.tensor_tensor(stats[i][:, 3, :], stats[i][:, 2, :], m_half[:], ALU.pow).then_inc(done, 1)

            def scaled_by_att(q):
                pool.wait_ge(emptied, through(pool_step(q, "U", 1)))
                pool.wait_ge(v_h, q(V_H, 3))
                pool.tensor_tensor(u_att[:], u_p[:, :, 2 * D:3 * D], att[:].unsqueeze(2).to_broadcast([P, TB, D]),
                                   ALU.mult).then_inc(g_h, 1)

            def first_root(q):
                pool.wait_ge(v_h, q(V_H, 10))
                root(0, g_h)

            def split_m2(q):
                zeros = zero[:].unsqueeze(2).to_broadcast([P, TB, D])
                pool.wait_ge(emptied, through(pool_step(q, "M2")))
                as_sum(m2_p[0][:], m2[:], zeros).then_inc(g_h, 1)
                pool.wait_ge(g_h, q(G_H, 3))
                pool.tensor_tensor(m2_r[:], m2[:], m2_p[0][:], ALU.subtract).then_inc(g_h, 1)
                pool.wait_ge(g_h, q(G_H, 4))
                as_sum(m2_p[1][:], m2_r[:], zeros).then_inc(g_h, 1)
                pool.wait_ge(g_h, q(G_H, 5))
                pool.tensor_tensor(m2_p[2][:], m2_r[:], m2_p[1][:], ALU.subtract).then_inc(g_h, 1)

            def cell(q):
                pool.wait_ge(a_o, q(A_O, 1))
                pool.tensor_tensor(h_minus_n[:], h[:], n_new[:], ALU.subtract).then_inc(g_o, 1)
                pool.tensor_tensor(h_plus_n[:], h[:], n_new[:], ALU.add).then_inc(g_o, 1)
                pool.wait_ge(g_o, q(G_O, 1))
                pool.tensor_tensor(z_part[:], h_minus_n[:], rz[:, :, D:2 * D], ALU.mult).then_inc(g_o, 1)

            def second_root(q):
                pool.wait_ge(v_o, q(V_O, 7))
                root(1, g_o)

            def pair(j):
                for (name, b, i), q in due(GPSIMD_STEPS, j):
                    if name == "SPLIT":
                        if not (b == 0 and isinstance(q.j, int) and q.j + q.lag == 0):
                            split_table(q, b, i)
                    elif name == "STAT":
                        statistics(q, b)
                    elif name == "WIDEN":
                        widen(q, b)
                    elif name == "ATT":
                        scaled_by_att(q)
                    elif name == "ROOT1":
                        first_root(q)
                    elif name == "M2S":
                        split_m2(q)
                    elif name == "CELL":
                        cell(q)
                    elif name == "ROOT2":
                        second_root(q)

            pool.wait_ge(v_pre, READY)
            for j in range(PAIRS[0], LOOP[0]):
                pair(j)
            with pool.Fori(LOOP[0], LOOP[-1] + 1) as j:
                pair(j)
            for j in range(LOOP[-1] + 1, PAIRS[-1] + 1):
                pair(j)


def kernel(x, adj, L0_gnn_W_pre, L0_gnn_b_pre, L0_gnn_W_post, L0_gnn_b_post, L1_gnn_W1, L1_gnn_b1,
           L1_gnn_W2, L1_gnn_b2, L1_gnn_W_ih, L1_gnn_b_ih, L1_gnn_W_hh, L1_gnn_b_hh):
    import ml_dtypes
    import concourse.bacc as bacc
    from concourse.bass_utils import run_bass_kernel_spmd

    given = [("x", x), ("adj", adj), ("w_pre", L0_gnn_W_pre), ("b_pre", L0_gnn_b_pre),
             ("w_post", L0_gnn_W_post), ("b_post", L0_gnn_b_post), ("w1", L1_gnn_W1), ("b1", L1_gnn_b1),
             ("w2", L1_gnn_W2), ("b2", L1_gnn_b2), ("w_ih", L1_gnn_W_ih), ("b_ih", L1_gnn_b_ih),
             ("w_hh", L1_gnn_W_hh), ("b_hh", L1_gnn_b_hh)]
    match_c, mbias_c = match_constants()
    constants = [("ident", np.eye(P, dtype=np.float32)), ("match", match_c.astype(ml_dtypes.bfloat16)),
                 ("mbias", mbias_c)]
    nc = bacc.Bacc("TRN2", target_bir_lowering=False, num_devices=1)
    arrays, args = {}, []
    for name, a in given + constants:
        a = np.ascontiguousarray(a)
        arrays[f"in_{name}"] = a
        args.append(nc.dram_tensor(f"in_{name}", a.shape, mybir.dt.from_np(a.dtype), kind="ExternalInput").ap())
    out = nc.dram_tensor("out", (B, N, D), F32, kind="ExternalOutput").ap()
    build(nc, *args, out)
    r = run_bass_kernel_spmd(nc, [arrays], core_ids=[0])
    return r.results[0]["out"]
```
